# Optimizing a Trainium2 kernel written in Bass

```python
import numpy as np
import jax
import jax.numpy as jnp

def _softmax(x, axis=-1):
    return jax.nn.softmax(x, axis=axis)

def _gelu(x):
    return jax.nn.gelu(x, approximate=True)

def _silu(x):
    return jax.nn.silu(x)

def _sigmoid(x):
    return jax.nn.sigmoid(x)

def _layernorm(x, axis=-1, eps=1e-05):
    m = jnp.mean(x, axis=axis, keepdims=True)
    v = jnp.var(x, axis=axis, keepdims=True)
    return (x - m) / jnp.sqrt(v + eps)

def _scatter_add(tgt, idx, src, axis=0):
    return tgt.at[idx].add(src)

def _segment_sum(src, seg, n):
    return jax.ops.segment_sum(src, seg, n)
kernel_name = 'mk_hybrid_d2_jaxref_r8_1e3b5b'

def setup_inputs(seed: int=0):
    np.random.seed(seed)
    _w = jnp.asarray

    def _L0_attn_a_setup():
        import jax, jax.numpy as jnp
        import numpy as np
        D_MODEL = 256
        N_HEADS = 16
        HEAD_DIM = D_MODEL // N_HEADS
        SCALE = HEAD_DIM ** (-0.5)
        key = jax.random.key(seed)
        ks = jax.random.split(key, 9)
        B, L, D = (4, 512, D_MODEL)
        s = 1.0 / np.sqrt(D)
        inp = {'x': jax.random.normal(ks[0], (B, L, D), dtype=jnp.float32)}
        inp['Wq'] = jax.random.normal(ks[1], (D, D), dtype=jnp.float32) * s
        inp['bq'] = jnp.zeros((D,), dtype=jnp.float32)
        inp['Wk'] = jax.random.normal(ks[2], (D, D), dtype=jnp.float32) * s
        inp['bk'] = jnp.zeros((D,), dtype=jnp.float32)
        inp['Wv'] = jax.random.normal(ks[3], (D, D), dtype=jnp.float32) * s
        inp['bv'] = jnp.zeros((D,), dtype=jnp.float32)
        inp['Wo'] = jax.random.normal(ks[4], (D, D), dtype=jnp.float32) * s
        inp['bo'] = jnp.zeros((D,), dtype=jnp.float32)
        return inp
    _L0_attn_a_in = _L0_attn_a_setup()

    def _L0_attn_b_setup():
        import jax, jax.numpy as jnp
        import numpy as np
        B, T, D = (2, 128, 256)
        H, DK, DV = (32, 48, 96)
        KD, VD = (H * DK, H * DV)
        CS = 4
        INTER = 704
        EPS = 1e-05

        def rmsnorm(x, w, eps=EPS):
            return x * jax.lax.rsqrt(jnp.mean(x * x, axis=-1, keepdims=True) + eps) * w

        def short_conv(x, w):
            K = w.shape[1]
            xp = jnp.pad(x, ((0, 0), (K - 1, 0), (0, 0)))
            out = sum((xp[:, k:k + x.shape[1], :] * w[:, k] for k in range(K)))
            return jax.nn.silu(out)

        def l2norm(x, eps=1e-06):
            return x * jax.lax.rsqrt(jnp.sum(x * x, axis=-1, keepdims=True) + eps)

        def gated_delta_rule(q, k, v, g, beta):
            scale = q.shape[-1] ** (-0.5)

            def step(S, inp):
                qt, kt, vt, gt, bt = inp
                S = S * jnp.exp(gt)[..., None, None]
                mem = jnp.einsum('bhk,bhkv->bhv', kt, S)
                delta = (vt - mem) * bt[..., None]
                S = S + jnp.einsum('bhk,bhv->bhkv', kt, delta)
                o = jnp.einsum('bhk,bhkv->bhv', qt * scale, S)
                return (S, o)
            S0 = jnp.zeros((q.shape[0], q.shape[2], q.shape[3], v.shape[3]), q.dtype)
            xs = (q.transpose(1, 0, 2, 3), k.transpose(1, 0, 2, 3), v.transpose(1, 0, 2, 3), g.transpose(1, 0, 2), beta.transpose(1, 0, 2))
            _, o = jax.lax.scan(step, S0, xs)
            return o.transpose(1, 0, 2, 3)
        key = jax.random.key(seed)
        ks = jax.random.split(key, 20)
        f = lambda k, sh, sc=0.02: jax.random.normal(k, sh, dtype=jnp.float32) * sc
        dt = jax.random.uniform(ks[7], (H,), minval=0.001, maxval=0.1)
        return dict(x=jax.random.normal(ks[0], (B, T, D), dtype=jnp.float32), rms1_w=jnp.ones((D,), jnp.float32), rms2_w=jnp.ones((D,), jnp.float32), Wq=f(ks[1], (D, KD)), Wk=f(ks[2], (D, KD)), Wv=f(ks[3], (D, VD)), Wa=f(ks[4], (D, H)), Wb=f(ks[5], (D, H)), Wg=f(ks[6], (D, VD)), dt_bias=jnp.log(jnp.expm1(dt)), A_log=jnp.log(jax.random.uniform(ks[8], (H,), minval=1.0, maxval=16.0)), conv_q_w=f(ks[9], (KD, CS), 0.5), conv_k_w=f(ks[10], (KD, CS), 0.5), conv_v_w=f(ks[11], (VD, CS), 0.5), gnorm_w=jnp.ones((DV,), jnp.float32), Wo=f(ks[12], (VD, D)), W1=f(ks[13], (D, INTER)), W3=f(ks[14], (D, INTER)), W2=f(ks[15], (INTER, D)))
    _L0_attn_b_in = _L0_attn_b_setup()

    def _L0_ffn_setup():
        import jax, jax.numpy as jnp
        import numpy as np
        EPS = 1e-08

        def _quantize(w):
            gamma = jnp.mean(jnp.abs(w))
            return jnp.clip(jnp.round(w / (gamma + EPS)), -1.0, 1.0)

        def _bitlinear(x, w):
            return jnp.matmul(x, _quantize(w).T)
        key = jax.random.key(seed)
        k1, k2, k3, k4 = jax.random.split(key, 4)
        d, h = (256, 704)
        x = jax.random.normal(k1, (4, 256, d), dtype=jnp.float32)
        w1 = jax.random.normal(k2, (h, d), dtype=jnp.float32)
        w2 = jax.random.normal(k3, (h, d), dtype=jnp.float32)
        w3 = jax.random.normal(k4, (d, h), dtype=jnp.float32)
        return {'x': x, 'w1': w1, 'w2': w2, 'w3': w3}
    _L0_ffn_in = _L0_ffn_setup()

    def _L1_attn_a_setup():
        import jax, jax.numpy as jnp
        import numpy as np
        E = 256
        H = 16
        D = E // H
        B = 4
        N = 256
        key = jax.random.key(seed)
        ks = jax.random.split(key, 5)
        scale_qkv = 1.0 / np.sqrt(E)
        scale_fc = 1.0 / np.sqrt(E)
        return {'x': jax.random.normal(ks[0], (B, N, E), dtype=jnp.float32), 'w_qkv': jax.random.uniform(ks[1], (E, E + 2 * D), jnp.float32, -scale_qkv, scale_qkv), 'b_qkv': jax.random.uniform(ks[2], (E + 2 * D,), jnp.float32, -scale_qkv, scale_qkv), 'w_fc': jax.random.uniform(ks[3], (E, E), jnp.float32, -scale_fc, scale_fc), 'b_fc': jax.random.uniform(ks[4], (E,), jnp.float32, -scale_fc, scale_fc)}
    _L1_attn_a_in = _L1_attn_a_setup()

    def _L1_attn_b_setup():
        import jax, jax.numpy as jnp
        import numpy as np
        H = 16
        NOPE = 64
        ROPE = 64
        QK = NOPE + ROPE
        VD = 128
        QR = 682
        KVR = 32
        D = 256
        THETA = 128000.0
        EPS = 1e-06

        def rmsnorm(x, w):
            var = jnp.mean(jnp.square(x.astype(jnp.float32)), axis=-1, keepdims=True)
            return (x * jax.lax.rsqrt(var + EPS)).astype(x.dtype) * w

        def _pair_permute(t):
            b, h, s, d = t.shape
            return t.reshape(b, h, s, d // 2, 2).swapaxes(-1, -2).reshape(b, h, s, d)

        def _rotate_half(t):
            t1, t2 = jnp.split(t, 2, axis=-1)
            return jnp.concatenate([-t2, t1], axis=-1)

        def _rope(q_pe, k_pe, seq_len):
            inv_freq = 1.0 / THETA ** (jnp.arange(0, ROPE, 2, dtype=jnp.float32) / ROPE)
            pos = jnp.arange(seq_len, dtype=jnp.float32)
            freqs = pos[:, None] * inv_freq[None, :]
            emb = jnp.concatenate([freqs, freqs], axis=-1)
            cos = jnp.cos(emb)[None, None]
            sin = jnp.sin(emb)[None, None]
            q_pe = _pair_permute(q_pe)
            k_pe = _pair_permute(k_pe)
            q_pe = q_pe * cos + _rotate_half(q_pe) * sin
            k_pe = k_pe * cos + _rotate_half(k_pe) * sin
            return (q_pe, k_pe)
        key = jax.random.key(seed)
        ks = jax.random.split(key, 8)
        s = 0.02
        return {'x': jax.random.normal(ks[0], (2, 256, D), dtype=jnp.float32), 'q_a_w': jax.random.normal(ks[1], (QR, D), dtype=jnp.float32) * s, 'q_a_ln': jnp.ones((QR,), dtype=jnp.float32), 'q_b_w': jax.random.normal(ks[2], (H * QK, QR), dtype=jnp.float32) * s, 'kv_a_w': jax.random.normal(ks[3], (KVR + ROPE, D), dtype=jnp.float32) * s, 'kv_a_ln': jnp.ones((KVR,), dtype=jnp.float32), 'kv_b_w': jax.random.normal(ks[4], (H * (NOPE + VD), KVR), dtype=jnp.float32) * s, 'o_w': jax.random.normal(ks[5], (D, H * VD), dtype=jnp.float32) * s}
    _L1_attn_b_in = _L1_attn_b_setup()

    def _L1_ffn_setup():
        import jax, jax.numpy as jnp
        import numpy as np
        B, S, D = (4, 512, 256)
        DFF = 4 * D
        CAPACITY = 0.125
        K = int(CAPACITY * S)
        key = jax.random.key(seed)
        ks = jax.random.split(key, 8)
        sc = 1.0 / np.sqrt(D)
        return {'x': jax.random.normal(ks[0], (B, S, D), dtype=jnp.float32), 'W_r': jax.random.normal(ks[1], (D, 1), dtype=jnp.float32) * sc, 'b_r': jnp.zeros((1,), dtype=jnp.float32), 'W1': jax.random.normal(ks[2], (D, DFF), dtype=jnp.float32) * sc, 'b1': jnp.zeros((DFF,), dtype=jnp.float32), 'W2': jax.random.normal(ks[3], (DFF, D), dtype=jnp.float32) * (1.0 / np.sqrt(DFF)), 'b2': jnp.zeros((D,), dtype=jnp.float32), 'position_ids': jnp.arange(B * S, dtype=jnp.int64 if jax.config.jax_enable_x64 else jnp.int32).reshape(B, S), 'cache_position': jnp.arange(S, dtype=jnp.int64 if jax.config.jax_enable_x64 else jnp.int32)}
    _L1_ffn_in = _L1_ffn_setup()
    _d = {'L0_attn_a_x': _L0_attn_a_in['x'], 'L0_attn_a_Wq': _L0_attn_a_in['Wq'], 'L0_attn_a_bq': _L0_attn_a_in['bq'], 'L0_attn_a_Wk': _L0_attn_a_in['Wk'], 'L0_attn_a_bk': _L0_attn_a_in['bk'], 'L0_attn_a_Wv': _L0_attn_a_in['Wv'], 'L0_attn_a_bv': _L0_attn_a_in['bv'], 'L0_attn_a_Wo': _L0_attn_a_in['Wo'], 'L0_attn_a_bo': _L0_attn_a_in['bo'], 'L0_attn_b_rms1_w': _L0_attn_b_in['rms1_w'], 'L0_attn_b_rms2_w': _L0_attn_b_in['rms2_w'], 'L0_attn_b_Wq': _L0_attn_b_in['Wq'], 'L0_attn_b_Wk': _L0_attn_b_in['Wk'], 'L0_attn_b_Wv': _L0_attn_b_in['Wv'], 'L0_attn_b_Wa': _L0_attn_b_in['Wa'], 'L0_attn_b_Wb': _L0_attn_b_in['Wb'], 'L0_attn_b_Wg': _L0_attn_b_in['Wg'], 'L0_attn_b_dt_bias': _L0_attn_b_in['dt_bias'], 'L0_attn_b_A_log': _L0_attn_b_in['A_log'], 'L0_attn_b_conv_q_w': _L0_attn_b_in['conv_q_w'], 'L0_attn_b_conv_k_w': _L0_attn_b_in['conv_k_w'], 'L0_attn_b_conv_v_w': _L0_attn_b_in['conv_v_w'], 'L0_attn_b_gnorm_w': _L0_attn_b_in['gnorm_w'], 'L0_attn_b_Wo': _L0_attn_b_in['Wo'], 'L0_attn_b_W1': _L0_attn_b_in['W1'], 'L0_attn_b_W3': _L0_attn_b_in['W3'], 'L0_attn_b_W2': _L0_attn_b_in['W2'], 'L0_ffn_w1': _L0_ffn_in['w1'], 'L0_ffn_w2': _L0_ffn_in['w2'], 'L0_ffn_w3': _L0_ffn_in['w3'], 'L1_attn_a_w_qkv': _L1_attn_a_in['w_qkv'], 'L1_attn_a_b_qkv': _L1_attn_a_in['b_qkv'], 'L1_attn_a_w_fc': _L1_attn_a_in['w_fc'], 'L1_attn_a_b_fc': _L1_attn_a_in['b_fc'], 'L1_attn_b_q_a_w': _L1_attn_b_in['q_a_w'], 'L1_attn_b_q_a_ln': _L1_attn_b_in['q_a_ln'], 'L1_attn_b_q_b_w': _L1_attn_b_in['q_b_w'], 'L1_attn_b_kv_a_w': _L1_attn_b_in['kv_a_w'], 'L1_attn_b_kv_a_ln': _L1_attn_b_in['kv_a_ln'], 'L1_attn_b_kv_b_w': _L1_attn_b_in['kv_b_w'], 'L1_attn_b_o_w': _L1_attn_b_in['o_w'], 'L1_ffn_W_r': _L1_ffn_in['W_r'], 'L1_ffn_b_r': _L1_ffn_in['b_r'], 'L1_ffn_W1': _L1_ffn_in['W1'], 'L1_ffn_b1': _L1_ffn_in['b1'], 'L1_ffn_W2': _L1_ffn_in['W2'], 'L1_ffn_b2': _L1_ffn_in['b2'], 'L1_ffn_position_ids': _L1_ffn_in['position_ids'], 'L1_ffn_cache_position': _L1_ffn_in['cache_position']}
    _x0 = _d['L0_attn_a_x']
    _d['L0_attn_a_x'] = jax.random.normal(jax.random.fold_in(jax.random.key(seed), 1), (4, 512, 256), dtype=_x0.dtype)
    del _x0
    return _d

def reference(L0_attn_a_x, L0_attn_a_Wq, L0_attn_a_bq, L0_attn_a_Wk, L0_attn_a_bk, L0_attn_a_Wv, L0_attn_a_bv, L0_attn_a_Wo, L0_attn_a_bo, L0_attn_b_rms1_w, L0_attn_b_rms2_w, L0_attn_b_Wq, L0_attn_b_Wk, L0_attn_b_Wv, L0_attn_b_Wa, L0_attn_b_Wb, L0_attn_b_Wg, L0_attn_b_dt_bias, L0_attn_b_A_log, L0_attn_b_conv_q_w, L0_attn_b_conv_k_w, L0_attn_b_conv_v_w, L0_attn_b_gnorm_w, L0_attn_b_Wo, L0_attn_b_W1, L0_attn_b_W3, L0_attn_b_W2, L0_ffn_w1, L0_ffn_w2, L0_ffn_w3, L1_attn_a_w_qkv, L1_attn_a_b_qkv, L1_attn_a_w_fc, L1_attn_a_b_fc, L1_attn_b_q_a_w, L1_attn_b_q_a_ln, L1_attn_b_q_b_w, L1_attn_b_kv_a_w, L1_attn_b_kv_a_ln, L1_attn_b_kv_b_w, L1_attn_b_o_w, L1_ffn_W_r, L1_ffn_b_r, L1_ffn_W1, L1_ffn_b1, L1_ffn_W2, L1_ffn_b2, L1_ffn_position_ids, L1_ffn_cache_position):

    def _L0_attn_a_ref(x, Wq, bq, Wk, bk, Wv, bv, Wo, bo):
        import jax, jax.numpy as jnp
        import numpy as np
        D_MODEL = 256
        N_HEADS = 16
        HEAD_DIM = D_MODEL // N_HEADS
        SCALE = HEAD_DIM ** (-0.5)
        B, L, D = x.shape
        H, Hd = (N_HEADS, HEAD_DIM)
        q = jnp.einsum('bld,ed->ble', x, Wq) + bq
        k = jnp.einsum('bld,ed->ble', x, Wk) + bk
        v = jnp.einsum('bld,ed->ble', x, Wv) + bv
        phi_q = jax.nn.elu(q) + 1.0
        phi_k = jax.nn.elu(k) + 1.0
        phi_q = phi_q.reshape(B, L, H, Hd)
        phi_k = phi_k.reshape(B, L, H, Hd)
        v = v.reshape(B, L, H, Hd)
        kv_sum = jnp.cumsum(phi_k * v, axis=1)
        context = (phi_q * kv_sum).reshape(B, L, D) * SCALE
        return jnp.einsum('bld,ed->ble', context, Wo) + bo

    def _L0_attn_b_ref(x, rms1_w, rms2_w, Wq, Wk, Wv, Wa, Wb, Wg, dt_bias, A_log, conv_q_w, conv_k_w, conv_v_w, gnorm_w, Wo, W1, W3, W2):
        import jax, jax.numpy as jnp
        import numpy as np
        B, T, D = (2, 128, 256)
        H, DK, DV = (32, 48, 96)
        KD, VD = (H * DK, H * DV)
        CS = 4
        INTER = 704
        EPS = 1e-05

        def rmsnorm(x, w, eps=EPS):
            return x * jax.lax.rsqrt(jnp.mean(x * x, axis=-1, keepdims=True) + eps) * w

        def short_conv(x, w):
            K = w.shape[1]
            xp = jnp.pad(x, ((0, 0), (K - 1, 0), (0, 0)))
            out = sum((xp[:, k:k + x.shape[1], :] * w[:, k] for k in range(K)))
            return jax.nn.silu(out)

        def l2norm(x, eps=1e-06):
            return x * jax.lax.rsqrt(jnp.sum(x * x, axis=-1, keepdims=True) + eps)

        def gated_delta_rule(q, k, v, g, beta):
            scale = q.shape[-1] ** (-0.5)

            def step(S, inp):
                qt, kt, vt, gt, bt = inp
                S = S * jnp.exp(gt)[..., None, None]
                mem = jnp.einsum('bhk,bhkv->bhv', kt, S)
                delta = (vt - mem) * bt[..., None]
                S = S + jnp.einsum('bhk,bhv->bhkv', kt, delta)
                o = jnp.einsum('bhk,bhkv->bhv', qt * scale, S)
                return (S, o)
            S0 = jnp.zeros((q.shape[0], q.shape[2], q.shape[3], v.shape[3]), q.dtype)
            xs = (q.transpose(1, 0, 2, 3), k.transpose(1, 0, 2, 3), v.transpose(1, 0, 2, 3), g.transpose(1, 0, 2), beta.transpose(1, 0, 2))
            _, o = jax.lax.scan(step, S0, xs)
            return o.transpose(1, 0, 2, 3)
        b, t, _ = x.shape
        h = rmsnorm(x, rms1_w)
        q = short_conv(h @ Wq, conv_q_w).reshape(b, t, H, DK)
        k = short_conv(h @ Wk, conv_k_w).reshape(b, t, H, DK)
        v = short_conv(h @ Wv, conv_v_w).reshape(b, t, H, DV)
        q, k = (l2norm(q), l2norm(k))
        g = -jnp.exp(A_log) * jax.nn.softplus(h @ Wa + dt_bias)
        beta = jax.nn.sigmoid(h @ Wb)
        o = gated_delta_rule(q, k, v, g, beta)
        gate = (h @ Wg).reshape(b, t, H, DV)
        o = rmsnorm(o, gnorm_w) * jax.nn.silu(gate)
        o = o.reshape(b, t, VD) @ Wo
        h2 = x + o
        ff = rmsnorm(h2, rms2_w)
        out = h2 + jax.nn.silu(ff @ W1) * (ff @ W3) @ W2
        return out

    def _L0_ffn_ref(x, w1, w2, w3):
        import jax, jax.numpy as jnp
        import numpy as np
        EPS = 1e-08

        def _quantize(w):
            gamma = jnp.mean(jnp.abs(w))
            return jnp.clip(jnp.round(w / (gamma + EPS)), -1.0, 1.0)

        def _bitlinear(x, w):
            return jnp.matmul(x, _quantize(w).T)
        x1 = _bitlinear(x, w1)
        x2 = _bitlinear(x, w2)
        hidden = jax.nn.sigmoid(x1) * x2
        return _bitlinear(hidden, w3)

    def _L1_attn_a_ref(x, w_qkv, b_qkv, w_fc, b_fc):
        import jax, jax.numpy as jnp
        import numpy as np
        E = 256
        H = 16
        D = E // H
        B = 4
        N = 256
        b, n, _ = x.shape
        qkv = x @ w_qkv + b_qkv
        q = qkv[..., :E].reshape(b, n, H, D)
        k = qkv[..., E:E + D]
        v = qkv[..., E + D:]
        scores = jnp.einsum('bnhd,bmd->bhnm', q, k) / jnp.sqrt(jnp.float32(D))
        causal = jnp.triu(jnp.ones((n, n), dtype=bool), k=1)
        scores = jnp.where(causal, -jnp.inf, scores)
        attn = jax.nn.softmax(scores, axis=-1)
        out = jnp.einsum('bhnm,bmd->bnhd', attn, v)
        out = out.reshape(b, n, E)
        return out @ w_fc + b_fc

    def _L1_attn_b_ref(x, q_a_w, q_a_ln, q_b_w, kv_a_w, kv_a_ln, kv_b_w, o_w):
        import jax, jax.numpy as jnp
        import numpy as np
        H = 16
        NOPE = 64
        ROPE = 64
        QK = NOPE + ROPE
        VD = 128
        QR = 682
        KVR = 32
        D = 256
        THETA = 128000.0
        EPS = 1e-06

        def rmsnorm(x, w):
            var = jnp.mean(jnp.square(x.astype(jnp.float32)), axis=-1, keepdims=True)
            return (x * jax.lax.rsqrt(var + EPS)).astype(x.dtype) * w

        def _pair_permute(t):
            b, h, s, d = t.shape
            return t.reshape(b, h, s, d // 2, 2).swapaxes(-1, -2).reshape(b, h, s, d)

        def _rotate_half(t):
            t1, t2 = jnp.split(t, 2, axis=-1)
            return jnp.concatenate([-t2, t1], axis=-1)

        def _rope(q_pe, k_pe, seq_len):
            inv_freq = 1.0 / THETA ** (jnp.arange(0, ROPE, 2, dtype=jnp.float32) / ROPE)
            pos = jnp.arange(seq_len, dtype=jnp.float32)
            freqs = pos[:, None] * inv_freq[None, :]
            emb = jnp.concatenate([freqs, freqs], axis=-1)
            cos = jnp.cos(emb)[None, None]
            sin = jnp.sin(emb)[None, None]
            q_pe = _pair_permute(q_pe)
            k_pe = _pair_permute(k_pe)
            q_pe = q_pe * cos + _rotate_half(q_pe) * sin
            k_pe = k_pe * cos + _rotate_half(k_pe) * sin
            return (q_pe, k_pe)
        B, S, _ = x.shape
        q = rmsnorm(x @ q_a_w.T, q_a_ln) @ q_b_w.T
        q = q.reshape(B, S, H, QK).transpose(0, 2, 1, 3)
        q_nope, q_pe = (q[..., :NOPE], q[..., NOPE:])
        ckv = x @ kv_a_w.T
        c, k_pe = (ckv[..., :KVR], ckv[..., KVR:])
        k_pe = k_pe[:, None, :, :]
        kv = rmsnorm(c, kv_a_ln) @ kv_b_w.T
        kv = kv.reshape(B, S, H, NOPE + VD).transpose(0, 2, 1, 3)
        k_nope, v = (kv[..., :NOPE], kv[..., NOPE:])
        q_pe, k_pe = _rope(q_pe, k_pe, S)
        query = jnp.concatenate([q_nope, q_pe], axis=-1)
        key = jnp.concatenate([k_nope, jnp.broadcast_to(k_pe, (B, H, S, ROPE))], axis=-1)
        scale = 1.0 / jnp.sqrt(jnp.float32(QK))
        scores = jnp.einsum('bhsd,bhtd->bhst', query, key) * scale
        attn = jax.nn.softmax(scores.astype(jnp.float32), axis=-1).astype(query.dtype)
        out = jnp.einsum('bhst,bhtd->bhsd', attn, v)
        out = out.transpose(0, 2, 1, 3).reshape(B, S, H * VD)
        return out @ o_w.T

    def _L1_ffn_ref(x, W_r, b_r, W1, b1, W2, b2, position_ids, cache_position):
        import jax, jax.numpy as jnp
        import numpy as np
        B, S, D = (4, 512, 256)
        DFF = 4 * D
        CAPACITY = 0.125
        K = int(CAPACITY * S)
        b, s, d = x.shape
        weights = jnp.einsum('bsd,do->bso', x, W_r).squeeze(-1) + b_r
        topk_vals, topk_idx = jax.lax.top_k(weights, K)
        threshold = topk_vals[:, -1]
        sel_mask = weights > threshold[:, None]
        xg = jnp.take_along_axis(x, topk_idx[..., None], axis=1)
        h = jax.nn.gelu(jnp.einsum('bkd,df->bkf', xg, W1) + b1)
        blk = jnp.einsum('bkf,fd->bkd', h, W2) + b2
        gate = (topk_vals > threshold[:, None]).astype(x.dtype)
        wg = jnp.take_along_axis(weights, topk_idx, axis=1)
        vals = blk * (wg * gate)[..., None]
        bidx = jnp.arange(b)[:, None]
        processed = jnp.zeros_like(x).at[bidx, topk_idx].add(vals)
        return processed + x * (~sel_mask)[..., None].astype(x.dtype)
    x = L0_attn_a_x
    x = x + _L0_attn_a_ref(_layernorm(x, axis=-1), L0_attn_a_Wq, L0_attn_a_bq, L0_attn_a_Wk, L0_attn_a_bk, L0_attn_a_Wv, L0_attn_a_bv, L0_attn_a_Wo, L0_attn_a_bo)
    x = x + _L0_ffn_ref(_layernorm(x, axis=-1), L0_ffn_w1, L0_ffn_w2, L0_ffn_w3)
    x = x + _L0_attn_b_ref(_layernorm(x, axis=-1), L0_attn_b_rms1_w, L0_attn_b_rms2_w, L0_attn_b_Wq, L0_attn_b_Wk, L0_attn_b_Wv, L0_attn_b_Wa, L0_attn_b_Wb, L0_attn_b_Wg, L0_attn_b_dt_bias, L0_attn_b_A_log, L0_attn_b_conv_q_w, L0_attn_b_conv_k_w, L0_attn_b_conv_v_w, L0_attn_b_gnorm_w, L0_attn_b_Wo, L0_attn_b_W1, L0_attn_b_W3, L0_attn_b_W2)
    x = x + _L0_ffn_ref(_layernorm(x, axis=-1), L0_ffn_w1, L0_ffn_w2, L0_ffn_w3)
    x = x + _L1_attn_a_ref(_layernorm(x, axis=-1), L1_attn_a_w_qkv, L1_attn_a_b_qkv, L1_attn_a_w_fc, L1_attn_a_b_fc)
    x = x + _L1_ffn_ref(_layernorm(x, axis=-1), L1_ffn_W_r, L1_ffn_b_r, L1_ffn_W1, L1_ffn_b1, L1_ffn_W2, L1_ffn_b2, L1_ffn_position_ids, L1_ffn_cache_position)
    x = x + _L1_attn_b_ref(_layernorm(x, axis=-1), L1_attn_b_q_a_w, L1_attn_b_q_a_ln, L1_attn_b_q_b_w, L1_attn_b_kv_a_w, L1_attn_b_kv_a_ln, L1_attn_b_kv_b_w, L1_attn_b_o_w)
    x = x + _L1_ffn_ref(_layernorm(x, axis=-1), L1_ffn_W_r, L1_ffn_b_r, L1_ffn_W1, L1_ffn_b1, L1_ffn_W2, L1_ffn_b2, L1_ffn_position_ids, L1_ffn_cache_position)
    return x

_drawn_inputs = setup_inputs


def setup_inputs(seed=0):
    import zlib

    import numpy as np

    out = dict(_drawn_inputs(seed))
    spreads = {'L0_attn_a_bq': (0.0, 0.1),
     'L0_attn_a_bk': (0.0, 0.1),
     'L0_attn_a_bv': (0.0, 0.1),
     'L0_attn_a_bo': (0.0, 0.1),
     'L0_attn_b_rms1_w': (1.0, 0.6),
     'L0_attn_b_rms2_w': (1.0, 0.6),
     'L0_attn_b_gnorm_w': (1.0, 0.6),
     'L1_attn_b_q_a_ln': (1.0, 0.6),
     'L1_attn_b_kv_a_ln': (1.0, 0.6),
     'L1_ffn_b1': (0.0, 0.8),
     'L1_ffn_b2': (0.0, 2.0)}
    factors = {'L0_attn_b_Wq': 8.0,
     'L0_attn_b_Wk': 8.0,
     'L0_attn_b_Wv': 8.0,
     'L0_attn_b_Wa': 8.0,
     'L0_attn_b_Wb': 8.0,
     'L0_attn_b_Wg': 8.0,
     'L0_attn_b_dt_bias': 8.0,
     'L0_attn_b_A_log': 8.0,
     'L0_attn_b_conv_q_w': 8.0,
     'L0_attn_b_conv_k_w': 8.0,
     'L0_attn_b_conv_v_w': 8.0,
     'L0_attn_b_Wo': 8.0,
     'L0_attn_b_W1': 8.0,
     'L0_attn_b_W3': 8.0,
     'L0_attn_b_W2': 8.0,
     'L1_attn_a_w_qkv': 8.0,
     'L1_attn_a_b_qkv': 8.0,
     'L1_attn_a_w_fc': 8.0,
     'L1_attn_a_b_fc': 64.0,
     'L1_attn_b_q_a_w': 8.0,
     'L1_attn_b_q_b_w': 8.0,
     'L1_attn_b_kv_a_w': 8.0,
     'L1_attn_b_kv_b_w': 8.0,
     'L1_attn_b_o_w': 8.0,
     'L1_ffn_W_r': 8.0,
     'L1_ffn_W1': 8.0,
     'L1_ffn_W2': 8.0}
    for name, (base, spread) in spreads.items():
        noise = np.random.default_rng([zlib.crc32(name.encode()), seed]).standard_normal(out[name].shape)
        drawn = base * np.exp(spread * noise) if base else spread * noise
        out[name] = jnp.asarray(drawn.astype(out[name].dtype))
    for name, factor in factors.items():
        out[name] = (out[name] * factor).astype(out[name].dtype)
    return out
```

```python
import concourse.bass as bass
from concourse import mybir
from contextlib import ExitStack

SEQ = 'AFBFCEDE'

B, L, D = 4, 512, 256
P = 128
NT = B * L // P
TB = L // P
KD = D // P
FH = 704
FJ = 6
FR = [min(P, FH - P * j) for j in range(FJ)]
DFF = 1024
EF = DFF // P
TOPK = L // 8

ARENA = 25800

f32 = mybir.dt.float32
bf16 = mybir.dt.bfloat16
ALU = mybir.AluOpType
ACT = mybir.ActivationFunctionType
AX = mybir.AxisListType


class Chain:

    def __init__(self, eng, sem):
        self.eng, self.sem, self.n, self.i, self.per, self.base = eng, sem, 0, None, 0, 0

    def __call__(self, ins):
        ins.then_inc(self.sem, 1)
        self.n += 1
        self.wait()

    def wait(self):
        if self.i is None:
            self.eng.wait_ge(self.sem, self.n)
        else:
            self.eng.wait_ge(self.sem, self.i * self.per + self.n)

    def enter(self, i, per):
        self.i, self.per, self.base = i, per, self.n

    def leave(self, count):
        assert self.n - self.base == self.per, (self.n - self.base, self.per)
        self.n, self.i = self.base + self.per * count, None


def build(nc, d, out):
    ctx = ExitStack()
    with ctx:
        def sb(name, shape, dt=f32):
            return ctx.enter_context(nc.sbuf_tensor(name, shape, dt))

        def sem(name):
            return ctx.enter_context(nc.semaphore(name))

        X = sb("X", [P, NT, D])
        XN = sb("XN", [P, NT, D])
        XT = sb("XT", [P, KD, B * L])
        ident = sb("ident", [P, P])
        ones = sb("ones", [P, 512])
        stats = sb("stats", [P, NT, 6])
        mv = sb("mv", [P, NT, 2])
        std = sb("std", [P, NT])
        rstd = sb("rstd", [P, NT])
        epsc = sb("epsc", [P, 8])
        arena = sb("arena", [P, ARENA])
        fold = sb("fold", [P, 4096])
        late = sb("late", [P, 4096])
        at = [0]

        def ar(*shape):
            n = 1
            for s in shape:
                n *= s
            v = arena[:, at[0]:at[0] + n]
            at[0] += n
            assert at[0] <= ARENA, at[0]
            if len(shape) == 2:
                v = v.rearrange("p (a b) -> p a b", a=shape[0])
            if len(shape) == 3:
                v = v.rearrange("p (a b c) -> p a b c", a=shape[0], b=shape[1])
            return v

        bank = [ctx.enter_context(nc.psum_tensor(f"bank{i}", [P, 512], f32)) for i in range(8)]

        s_x0 = sem("x_loaded")
        s_const = sem("constants_loaded")
        s_x = sem("x_tiles_updated")
        s_lnst = sem("ln_stats")
        s_lnmv = sem("ln_variances")
        s_lnstd = sem("ln_deviations")
        s_xn = sem("ln_tiles_normalised")
        s_xtp = sem("ln_transposed_psum")
        s_xt = sem("ln_transposed")
        s_dve = sem("vector_chain")
        s_act = sem("scalar_chain")
        s_out = sem("out_stored")
        block = ctx.enter_context(nc.Block())
        W = {}
        plan = []
        for si, kind in enumerate(SEQ):
            plan.append((si, kind, SEQ[:si].count(kind)))
        loads = []

        def ld(name, dst, src, s):
            loads.append((dst, src, s))

        ld("ones", ones[:, :], d["ones"], s_const)
        ld("ident", ident[:, :], d["ident"], s_const)
        ld("eps", epsc[:, :], d["eps"], s_const)

        norms = []

        def norm_vector(dve, n, ready, src, dst, rms=False, eps=0):
            if ready:
                dve.wait_ge(s_x, ready)
            else:
                dve.wait_ge(s_x0, 16)
            for t in range(NT):
                last = nc.vector.bn_stats(stats[:, t, :], src[:, t, :])
            last.then_inc(s_lnst, 1)
            dve.wait_ge(s_lnst, n[1] + 1)
            for t in range(NT):
                last = nc.vector.bn_aggr(mv[:, t, :], stats[:, t, :])
            if rms:
                n_sq = n[1] + 2
                last.then_inc(s_lnst, 1)
                dve.wait_ge(s_lnst, n_sq)
                nc.vector.tensor_tensor(rstd[:, :], mv[:, :, 0], mv[:, :, 0], ALU.mult).then_inc(s_lnst, 1)
                dve.wait_ge(s_lnst, n_sq + 1)
                last = nc.vector.tensor_tensor(mv[:, :, 1], mv[:, :, 1], rstd[:, :], ALU.add)
            last.then_inc(s_lnmv, 1)
            dve.wait_ge(s_lnstd, n[0] + 1)
            nc.vector.reciprocal(rstd[:, :], std[:, :]).then_inc(s_lnst, 1)
            dve.wait_ge(s_lnst, n[1] + (4 if rms else 2))
            for t in range(NT):
                if rms:
                    nc.vector.tensor_scalar(dst[:, t, :], src[:, t, :], rstd[:, t:t + 1], None,
                                            ALU.mult).then_inc(s_xn, 1)
                else:
                    nc.vector.tensor_scalar(dst[:, t, :], src[:, t, :], mv[:, t, 0:1], rstd[:, t:t + 1],
                                            ALU.subtract, ALU.mult).then_inc(s_xn, 1)

        def norm_scalar(act, n, eps_col):
            act.wait_ge(s_lnmv, n[0] + 1)
            nc.scalar.activation(std[:, :], mv[:, :, 1], ACT.Sqrt, bias=epsc[:, eps_col:eps_col + 1],
                                 scale=1.0).then_inc(s_lnstd, 1)

        def transpose_tensor(pe, n, src, ready=None):
            for g in range(8):
                q, k = g // 2, g % 2
                if ready is None:
                    pe.wait_ge(s_xn, 16 * n[0] + 4 * (q + 1))
                elif g == 0:
                    pe.wait_ge(*ready)
                if g >= 2:
                    pe.wait_ge(s_xt, 8 * n[2] + g - 1)
                for t in range(4):
                    last = nc.tensor.transpose(bank[6 + k][:, t * P:(t + 1) * P],
                                               src[:, 4 * q + t, k * P:(k + 1) * P], ident[:, :])
                last.then_inc(s_xtp, 1)
            pe.wait_ge(s_xt, 8 * n[2] + 8)

        def transpose_scalar(act, n, scale=None):
            for g in range(8):
                q, k = g // 2, g % 2
                act.wait_ge(s_xtp, 8 * n[2] + g + 1)
                if scale is None:
                    nc.scalar.activation(XT[:, k, q * 512:(q + 1) * 512], bank[6 + k][:, :],
                                         ACT.Copy).then_inc(s_xt, 1)
                else:
                    nc.scalar.activation(XT[:, k, q * 512:(q + 1) * 512], bank[6 + k][:, :],
                                         ACT.Copy, scale=scale[:, k:k + 1]).then_inc(s_xt, 1)

        NRM = {}
        cn, cs, ct = 0, 0, 0
        GLU = {si: sum(kk in 'FB' for kk in SEQ[:si]) for si in range(len(SEQ))}
        for si, kind, _ in plan:
            NRM[si] = (cn, cs, ct)
            if kind == 'B':
                NRM[si, 1] = (cn + 1, cs + 2, ct)
                NRM[si, 2] = (cn + 2, cs + 6, ct + 1)
                cn, cs, ct = cn + 3, cs + 10, ct + 2
            elif kind == 'C':
                NRM[si, 1] = (cn + 1, cs + 2, ct + 1)
                cn, cs, ct = cn + 1, cs + 2, ct + 2
            elif kind == 'E':
                cn, cs = cn + 1, cs + 2
            else:
                cn, cs, ct = cn + 1, cs + 2, ct + 1

        if 'A' in SEQ:
            at[0] = 0
            sA_w = sem("A_weights")
            sA_ps = sem("A_projected")
            sA_relu = sem("A_relu")
            sA_min = sem("A_min")
            sA_exp = sem("A_exp")
            sA_kv = sem("A_kv")
            sA_ct = sem("A_context")
            sA_po = sem("A_output")
            sA_bo = sem("A_bias")
            wqkv = ar(3, KD, D)
            wo_a = ar(KD, D)
            bqkv = ar(3, KD)
            bo_a = ar(D)
            ld("A_wqkv", wqkv[:, :, :, :], d["A_wqkv"].rearrange("m (k p) e -> p m k e", p=P), sA_w)
            ld("A_wo", wo_a[:, :, :], d["A_wo"].rearrange("(k p) e -> p k e", p=P), sA_w)
            ld("A_b", bqkv[:, :, :], d["A_b"], sA_w)
            ld("A_bo", bo_a[:, :], d["A_bo"].partition_broadcast(P), sA_w)
            RQ, RK, MQ, MK = ar(2, 512), ar(2, 512), ar(2, 512), ar(2, 512)
            PQ, PK, KV, CS = ar(2, 512), ar(2, 512), ar(2, 512), ar(2, 512)
            CT = ar(KD, B * L)

            def A_tensor(pe, si, inst):
                def project(u):
                    b, e = u // 2, u % 2
                    if u >= 2:
                        pe.wait_ge(sA_relu, u - 1)
                        pe.wait_ge(sA_kv, u - 1)
                    for m in range(3):
                        for k in range(KD):
                            last = nc.tensor.matmul(bank[3 * (u % 2) + m][:, :], wqkv[:, m, k, e * P:(e + 1) * P],
                                                    XT[:, k, b * L:(b + 1) * L], start=k == 0, stop=k == KD - 1)
                    last.then_inc(sA_ps, 1)

                transpose_tensor(pe, NRM[si], XN)
                pe.wait_ge(sA_w, 64)
                for u in range(4):
                    project(u)
                for b in range(B):
                    pe.wait_ge(sA_ct, 2 * b + 2)
                    for t in range(TB):
                        T = TB * b + t
                        if T >= 2:
                            pe.wait_ge(s_x, NT * si + T - 1)
                        for k in range(KD):
                            last = nc.tensor.matmul(bank[6 + T % 2][:, 0:D], CT[:, k, T * P:(T + 1) * P],
                                                    wo_a[:, k, :], start=k == 0, stop=k == KD - 1)
                        last.then_inc(sA_po, 1)
                    if b < 2:
                        project(2 * b + 4)
                        project(2 * b + 5)

            def A_scalar(act, si, inst):
                norm_scalar(act, NRM[si], 0)
                transpose_scalar(act, NRM[si])
                act.wait_ge(sA_w, 64)
                for u in range(8):
                    e = u % 2
                    act.wait_ge(sA_ps, u + 1)
                    if u >= 2:
                        act.wait_ge(sA_kv, u - 1)
                    nc.scalar.activation(RQ[:, u % 2, :], bank[3 * (u % 2)][:, :], ACT.Relu,
                                         bias=bqkv[:, 0, e:e + 1], scale=1.0)
                    nc.scalar.activation(RK[:, u % 2, :], bank[3 * (u % 2) + 1][:, :], ACT.Relu,
                                         bias=bqkv[:, 1, e:e + 1], scale=1.0).then_inc(sA_relu, 1)
                    act.wait_ge(sA_min, u + 1)
                    nc.scalar.activation(MQ[:, u % 2, :], MQ[:, u % 2, :], ACT.Exp)
                    nc.scalar.activation(MK[:, u % 2, :], MK[:, u % 2, :], ACT.Exp).then_inc(sA_exp, 1)

            def A_gpsimd(pool, si, inst):
                pool.wait_ge(sA_w, 64)
                pool.wait_ge(s_xn, NT * (NRM[si][0] + 1))
                for t in range(NT):
                    last = nc.gpsimd.tensor_tensor(X[:, t, :], X[:, t, :], bo_a[:, :], ALU.add)
                last.then_inc(sA_bo, 1)

            def A_vector(dve, si, inst, link):
                def low(u):
                    e = u % 2
                    dve.wait_ge(sA_relu, u + 1)
                    if u >= 2:
                        dve.wait_ge(sA_exp, u - 1)
                    nc.vector.tensor_scalar(MQ[:, u % 2, :], bank[3 * (u % 2)][:, :], bqkv[:, 0, e:e + 1], 0.0,
                                            ALU.add, ALU.min)
                    nc.vector.tensor_scalar(MK[:, u % 2, :], bank[3 * (u % 2) + 1][:, :], bqkv[:, 1, e:e + 1], 0.0,
                                            ALU.add, ALU.min).then_inc(sA_min, 1)

                def add(b):
                    if b == 0:
                        dve.wait_ge(sA_bo, 1)
                    for t in range(TB):
                        T = TB * b + t
                        dve.wait_ge(sA_po, T + 1)
                        nc.vector.tensor_tensor(X[:, T, :], X[:, T, :], bank[6 + T % 2][:, 0:D],
                                                ALU.add).then_inc(s_x, 1)

                norm_vector(dve, NRM[si], NT * si, X, XN)
                dve.wait_ge(sA_w, 64)
                low(0)
                for u in range(8):
                    b, e, r = u // 2, u % 2, u % 2
                    if u in (3, 5):
                        add((u - 3) // 2)
                    if u < 7:
                        low(u + 1)
                    dve.wait_ge(sA_exp, u + 1)
                    nc.vector.tensor_tensor(PQ[:, r, :], MQ[:, r, :], RQ[:, r, :], ALU.add)
                    link(nc.vector.tensor_tensor(PK[:, r, :], MK[:, r, :], RK[:, r, :], ALU.add))
                    nc.vector.scalar_tensor_tensor(KV[:, r, :], bank[3 * r + 2][:, :], bqkv[:, 2, e:e + 1],
                                                   PK[:, r, :], ALU.add, ALU.mult).then_inc(sA_kv, 1)
                    dve.wait_ge(sA_kv, u + 1)
                    link(nc.vector.tensor_tensor_scan(CS[:, r, :], ones[:, :], KV[:, r, :], 0.0,
                                                      ALU.mult, ALU.add))
                    nc.vector.scalar_tensor_tensor(CT[:, e, b * L:(b + 1) * L], PQ[:, r, :], 0.25,
                                                   CS[:, r, :], ALU.mult, ALU.mult).then_inc(sA_ct, 1)
                add(2)
                add(3)

            W['A'] = dict(scalar=A_scalar, vector=A_vector, tensor=A_tensor, gpsimd=A_gpsimd)

        if 'F' in SEQ or 'B' in SEQ:
            at[0] = 0
            sF_w = sem("F_weights")
            sF_abs = sem("F_abs_sums")
            sF_sum = sem("F_totals")
            sF_q = sem("F_quantised")
            sF_ps = sem("F_projected")
            sF_sig = sem("F_gated")
            sF_h = sem("F_hidden")
            sF_po = sem("F_output")
            w12 = sb("F_w12", [P, 2, KD, FH])
            w3 = sb("F_w3", [P, FJ, D])
            gsum = sb("F_gsum", [P, 3])
            thr = sb("F_thr", [P, 3])
            nthr = sb("F_nthr", [P, 3])
            ld("F_w12", w12[:, :, :, :], d["F_w12"].rearrange("m (k p) e -> p m k e", p=P), sF_w)
            ld("F_w3", w3[:, :, :], d["F_w3"].rearrange("(j p) e -> p j e", p=P), sF_w)
            gate_sig = ar(2, 512)
            H = ar(2, FJ, 512)
            QS = ar(2, 2 * FH)
            w_flat = [w12[:, 0, :, :].rearrange("p k e -> p (k e)"), w12[:, 1, :, :].rearrange("p k e -> p (k e)"),
                      w3[:, :, :].rearrange("p j e -> p (j e)")]

            def F_tensor(pe, si, inst):
                transpose_tensor(pe, NRM[si], XN)
                if inst == 0:
                    pe.wait_ge(sF_abs, 3)
                    nc.tensor.matmul(bank[4][:, 0:3], ones[:, 0:P], gsum[:, :], start=True,
                                     stop=True).then_inc(sF_sum, 1)
                    pe.wait_ge(sF_q, 3)
                glu_tensor(pe, si, GLU[si], w12, w3)

            def glu_tensor(pe, si, inst, w12, w3):
                iu = 24 * inst

                def project(n):
                    for j in range(FJ):
                        u = FJ * n + j
                        if u >= 2:
                            pe.wait_ge(sF_h, iu + u - 1)
                        for m in range(2):
                            for k in range(KD):
                                last = nc.tensor.matmul(bank[2 * (u % 2) + m][0:FR[j], :],
                                                        w12[:, m, k, j * P:j * P + FR[j]],
                                                        XT[:, k, n * 512:(n + 1) * 512],
                                                        start=k == 0, stop=k == KD - 1)
                        last.then_inc(sF_ps, 1)

                project(0)
                for n in range(B):
                    if n + 1 < B:
                        project(n + 1)
                    pe.wait_ge(sF_h, iu + FJ * (n + 1))
                    for t in range(TB):
                        T = TB * n + t
                        if T >= 2:
                            pe.wait_ge(s_x, NT * si + T - 1)
                        for j in range(FJ):
                            last = nc.tensor.matmul(bank[4 + T % 2][:, 0:D], H[0:FR[j], n % 2, j * 512 + t * P:j * 512 + (t + 1) * P],
                                                    w3[0:FR[j], j, :], start=j == 0, stop=j == FJ - 1)
                        last.then_inc(sF_po, 1)

            def F_scalar(act, si, inst):
                norm_scalar(act, NRM[si], 0)
                if inst == 0:
                    act.wait_ge(sF_w, 32)
                    for m in range(3):
                        n = 3 * D * 2 if m == 2 else 2 * FH
                        nc.scalar.activation(QS[:, m % 2, 0:min(n, 2 * FH)] if m < 2 else H3, w_flat[m],
                                             ACT.Abs, accum_out=gsum[:, m:m + 1]).then_inc(sF_abs, 1)
                transpose_scalar(act, NRM[si])
                glu_scalar(act, GLU[si], ACT.Sigmoid)

            def glu_scalar(act, inst, func):
                for u in range(24):
                    r = FR[u % FJ]
                    act.wait_ge(sF_ps, 24 * inst + u + 1)
                    if u >= 2:
                        act.wait_ge(sF_h, 24 * inst + u - 1)
                    nc.scalar.activation(gate_sig[0:r, u % 2, :], bank[2 * (u % 2)][0:r, :], func).then_inc(sF_sig, 1)

            def F_vector(dve, si, inst, link):
                norm_vector(dve, NRM[si], NT * si, X, XN)
                if inst == 0:
                    dve.wait_ge(sF_sum, 1)
                    nc.vector.tensor_scalar(thr[:, :], bank[4][:, 0:3], 0.5 / (FH * D), 0.5e-8, ALU.mult, ALU.add)
                    link(nc.vector.tensor_scalar(nthr[:, :], bank[4][:, 0:3], -0.5 / (FH * D), -0.5e-8, ALU.mult, ALU.add))
                    for m in range(3):
                        low = H3 if m == 2 else QS[:, m, :]
                        link(nc.vector.tensor_scalar(low, w_flat[m], nthr[:, m:m + 1], None, ALU.is_lt))
                        nc.vector.scalar_tensor_tensor(w_flat[m], w_flat[m], thr[:, m:m + 1], low,
                                                       ALU.is_gt, ALU.subtract).then_inc(sF_q, 1)

                glu_vector(dve, GLU[si])

            def glu_vector(dve, inst):
                def add(n):
                    for t in range(TB):
                        T = TB * n + t
                        dve.wait_ge(sF_po, NT * inst + T + 1)
                        nc.vector.tensor_tensor(X[:, T, :], X[:, T, :], bank[4 + T % 2][:, 0:D],
                                                ALU.add).then_inc(s_x, 1)

                for n in range(B):
                    for j in range(FJ):
                        u, r = FJ * n + j, FR[j]
                        dve.wait_ge(sF_sig, 24 * inst + u + 1)
                        nc.vector.tensor_tensor(H[0:r, n % 2, j * 512:(j + 1) * 512], gate_sig[0:r, u % 2, :],
                                                bank[2 * (u % 2) + 1][0:r, :], ALU.mult).then_inc(sF_h, 1)
                    if n:
                        add(n - 1)
                add(B - 1)

            H = H.rearrange("p n j t -> p n (j t)")
            H3 = H[:, 0, 0:FJ * D]
            W['F'] = dict(scalar=F_scalar, vector=F_vector, tensor=F_tensor)

        if 'E' in SEQ:
            at[0] = 0
            sE_w = sem("E_weights")
            sE_rt = sem("E_router_scores")
            sE_pe = sem("E_router_and_gather_psum")
            sE_act = sem("E_router_and_gather_copied")
            sE_slot = sem("E_slots")
            sE_pick = sem("E_pick_matrices")
            sE_ptp = sem("E_picks_transposed_psum")
            sE_pt = sem("E_picks_transposed")
            sE_hp = sem("E_hidden_psum")
            sE_h = sem("E_hidden")
            sE_bp = sem("E_block_psum")
            sE_bk = sem("E_block")
            sE_sc = sem("E_scattered")
            eW1 = late[:, 0:KD * DFF].rearrange("p (k c) -> p k c", k=KD)
            eW2 = late[:, KD * DFF:].rearrange("p (f c) -> p f c", f=EF)
            eb1 = sb("E_b1", [P, EF])
            eb2 = sb("E_b2", [P, D])
            ewr = sb("E_wr", [P, D])
            ebr = sb("E_br", [P, 1])
            iota = sb("E_iota", [P, P])
            eoff = sb("E_off", [B, 1])
            ld("E3", eb1[:, :], d["E_b1"], sE_w)
            ld("E4", eb2[:, :], d["E_b2"].partition_broadcast(P), sE_w)
            ld("E5", ewr[:, :], d["E_Wr"].partition_broadcast(P), sE_w)
            ld("E6", ebr[:, :], d["E_br"].partition_broadcast(P), sE_w)
            ld("E7", iota[:, :], d["iota"].partition_broadcast(P), sE_w)
            ld("E8", eoff[:, :], d["E_off"], sE_w)
            wt = ar(B, TB)
            wt2 = wt.rearrange("p b t -> p (b t)")
            W4, Wa, Wb = ar(512)[0:B], ar(512)[0:B], ar(512)[0:B]
            m8 = ar(8)[0:B]
            msk, csm, slot = ar(512)[0:B], ar(512)[0:B], ar(512)[0:B]
            slt = ar(TB, B)
            nsel = ar(TB, B)
            PK_ = ar(NT, P)
            PT = ar(NT, P)
            XG = ar(KD, 256)
            HG = ar(EF, 256)
            BK = ar(2, D)
            junk = ar(NT, D)

            def E_sync(sp, si, inst):
                if inst == 0:
                    sp.dma_start(eW1, d["E_W1"].rearrange("(k p) e -> p k e", p=P)).then_inc(sE_w, 16)
                    sp.dma_start(eW2, d["E_W2"].rearrange("(k p) e -> p k e", p=P)).then_inc(sE_w, 16)

            def E_tensor(pe, si, inst):
                pe.wait_ge(sE_w, 128)
                pe.wait_ge(sE_rt, inst + 1)
                for t in range(TB):
                    last = nc.tensor.transpose(bank[0][0:B, t * P:(t + 1) * P], wt[:, :, t], ident[:, :])
                last.then_inc(sE_pe, 1)
                pe.wait_ge(sE_slot, inst + 1)
                for t in range(TB):
                    last = nc.tensor.transpose(bank[1][:, t * B:(t + 1) * B], slot[:, t * P:(t + 1) * P],
                                               ident[0:B, 0:B])
                last.then_inc(sE_pe, 1)
                pe.wait_ge(sE_pick, NT * inst + NT)
                for k in range(KD):
                    for s in range(2):
                        for j in range(8):
                            T = 8 * s + j
                            last = nc.tensor.matmul(bank[0][:, k * 256 + s * P:k * 256 + (s + 1) * P],
                                                    XN[:, T, k * P:(k + 1) * P], PK_[:, T, :],
                                                    start=j == 0, stop=j == 7)
                last.then_inc(sE_pe, 1)
                for q in range(4):
                    for t in range(4):
                        last = nc.tensor.transpose(bank[2 + q][:, t * P:(t + 1) * P], PK_[:, 4 * q + t, :], ident[:, :])
                    last.then_inc(sE_ptp, 1)
                pe.wait_ge(sE_act, 3 * inst + 3)
                for f in range(EF):
                    if f >= 2:
                        pe.wait_ge(sE_h, EF * inst + f - 1)
                    for k in range(KD):
                        last = nc.tensor.matmul(bank[6 + f % 2][:, 0:256], eW1[:, k, f * P:(f + 1) * P], XG[:, k, :],
                                                start=k == 0, stop=k == KD - 1)
                    last.then_inc(sE_hp, 1)
                pe.wait_ge(sE_h, EF * inst + EF)
                for s in range(2):
                    for f in range(EF):
                        last = nc.tensor.matmul(bank[s][:, 0:D], HG[:, f, s * P:(s + 1) * P], eW2[:, f, :],
                                                start=f == 0, stop=f == EF - 1)
                    last.then_inc(sE_bp, 1)
                pe.wait_ge(sE_pt, 4 * inst + 4)
                pe.wait_ge(sE_bk, 2 * inst + 2)
                for T in range(NT):
                    if T >= 4:
                        pe.wait_ge(s_x, NT * si + T - 3)
                    nc.tensor.matmul(bank[2 + T % 4][:, 0:D], PT[:, T, :], BK[:, T // 8, :],
                                     start=True, stop=True).then_inc(sE_sc, 1)

            def E_scalar(act, si, inst):
                norm_scalar(act, NRM[si], 0)
                act.wait_ge(sE_pe, 3 * inst + 1)
                nc.scalar.activation(W4, bank[0][0:B, :], ACT.Copy).then_inc(sE_act, 1)
                act.wait_ge(sE_pe, 3 * inst + 2)
                nc.scalar.activation(slt.rearrange("p t b -> p (t b)"), bank[1][:, 0:NT], ACT.Copy).then_inc(sE_act, 1)
                act.wait_ge(sE_pe, 3 * inst + 3)
                nc.scalar.activation(XG.rearrange("p k s -> p (k s)"), bank[0][:, :], ACT.Copy).then_inc(sE_act, 1)
                for q in range(4):
                    act.wait_ge(sE_ptp, 4 * inst + q + 1)
                    nc.scalar.activation(PT[:, 4 * q:4 * q + 4, :].rearrange("p t s -> p (t s)"), bank[2 + q][:, :],
                                         ACT.Copy).then_inc(sE_pt, 1)
                act.wait_ge(sE_w, 128)
                for f in range(EF):
                    act.wait_ge(sE_hp, EF * inst + f + 1)
                    nc.scalar.activation(HG[:, f, :], bank[6 + f % 2][:, 0:256], ACT.Gelu_apprx_tanh,
                                         bias=eb1[:, f:f + 1], scale=1.0).then_inc(sE_h, 1)

            def E_vector(dve, si, inst, link):
                norm_vector(dve, NRM[si], NT * si, X, XN)
                dve.wait_ge(sE_w, 128)
                dve.wait_ge(s_xn, NT * (NRM[si][0] + 1))
                for t in range(NT):
                    last = nc.vector.tensor_tensor_reduce(out=junk[:, t, :], in0=XN[:, t, :], in1=ewr[:, :],
                                                          scale=1.0, scalar=0.0, op0=ALU.mult, op1=ALU.add,
                                                          accum_out=wt2[:, t:t + 1])
                link(last)
                nc.vector.tensor_scalar(wt2, wt2, ebr[:, 0:1], None, ALU.add).then_inc(sE_rt, 1)
                dve.wait_ge(sE_act, 3 * inst + 1)
                src, nxt = W4, Wa
                for r in range(TOPK // 8):
                    link(nc.vector.max(m8, src))
                    if r < TOPK // 8 - 1:
                        link(nc.vector.match_replace(nxt, m8, src, -3.0e38))
                        src, nxt = nxt, (Wb if nxt is Wa else Wa)
                link(nc.vector.tensor_scalar(msk, W4, m8[:, 7:8], None, ALU.is_gt))
                link(nc.vector.tensor_tensor_scan(csm, ones[0:B, :], msk, 0.0, ALU.mult, ALU.add))
                link(nc.vector.scalar_tensor_tensor(slot, csm, eoff[:, 0:1], msk, ALU.add, ALU.mult))
                nc.vector.tensor_scalar(slot, slot, -1.0, None, ALU.add).then_inc(sE_slot, 1)
                dve.wait_ge(sE_act, 3 * inst + 2)
                for T in range(NT):
                    b, t = T // TB, T % TB
                    nc.vector.tensor_scalar(PK_[:, T, :], iota[:, :], slt[:, t, b:b + 1], None,
                                            ALU.is_equal).then_inc(sE_pick, 1)
                link(nc.vector.tensor_scalar(nsel, slt, 0.0, None, ALU.is_lt))
                for T in range(NT):
                    b, t = T // TB, T % TB
                    last = nc.vector.scalar_tensor_tensor(X[:, T, :], XN[:, T, :], nsel[:, t, b:b + 1], X[:, T, :],
                                                          ALU.mult, ALU.add)
                link(last)
                for s in range(2):
                    dve.wait_ge(sE_bp, 2 * inst + s + 1)
                    nc.vector.tensor_tensor(BK[:, s, :], eb2[:, :], bank[s][:, 0:D], ALU.add).then_inc(sE_bk, 1)
                for T in range(NT):
                    b, t = T // TB, T % TB
                    dve.wait_ge(sE_sc, NT * inst + T + 1)
                    nc.vector.scalar_tensor_tensor(X[:, T, :], bank[2 + T % 4][:, 0:D], wt[:, b, t:t + 1], X[:, T, :],
                                                   ALU.mult, ALU.add).then_inc(s_x, 1)

            W['E'] = dict(sync=E_sync, scalar=E_scalar, vector=E_vector, tensor=E_tensor)

        def attention(name, units, w_of, row_of):
            NU, NG = units, units // 4
            s_s, s_sm, s_p = sem(name + "_scores"), sem(name + "_scaled"), sem(name + "_probs")
            s_t, s_pta, s_ptv = sem(name + "_probs_turned_psum"), sem(name + "_turned_by_scalar"), sem(name + "_turned_by_vector")
            s_pv, s_o = sem(name + "_values_mixed"), sem(name + "_groups_done")
            SM, PR, PTs = ar(4, 512), ar(4, 512), ar(4, 512)
            nb, rsum, rinv, tick = ar(NU), ar(NU), ar(NU), ar(NU)
            TLAG, VLAG = 2, 4

            def scores_tensor(pe, lap, score, value_rhs, dv):
                def turn(u):
                    pe.wait_ge(s_p, lap * NU + u + 1)
                    if u >= 2:
                        if u % 2 == 0:
                            pe.wait_ge(s_pta, lap * (NU // 2) + u // 2)
                        else:
                            pe.wait_ge(s_ptv, lap * (NU // 2) + u // 2)
                    for m in range(w_of(u)):
                        last = nc.tensor.transpose(bank[4 + u % 2][:, m * P:(m + 1) * P],
                                                   PR[:, u % 4, m * P:(m + 1) * P], ident[:, :])
                    last.then_inc(s_t, 1)

                def mix(u):
                    if u % 2 == 0:
                        pe.wait_ge(s_pta, lap * (NU // 2) + u // 2 + 1)
                    else:
                        pe.wait_ge(s_ptv, lap * (NU // 2) + u // 2 + 1)
                    g, q = u // 4, u % 4
                    if q == 0 and g >= 2:
                        pe.wait_ge(s_o, lap * NG + g)
                    for m in range(w_of(u)):
                        last = nc.tensor.matmul(bank[6 + g % 2][:, q * dv:(q + 1) * dv],
                                                PTs[:, u % 4, m * P:(m + 1) * P], value_rhs(u, m),
                                                start=m == 0, stop=m == w_of(u) - 1)
                    if q == 3:
                        last.then_inc(s_pv, 1)

                for i in range(NU + VLAG):
                    if i < NU:
                        if i >= 4:
                            pe.wait_ge(s_sm, lap * NU + i - 3)
                        score(i, bank[i % 4][:, 0:w_of(i) * P]).then_inc(s_s, 1)
                    if TLAG <= i < NU + TLAG:
                        turn(i - TLAG)
                    if VLAG <= i:
                        mix(i - VLAG)

            def scores_scalar(act, lap):
                def turned(u):
                    act.wait_ge(s_t, lap * NU + u + 1)
                    if u >= 4:
                        act.wait_ge(s_t, lap * NU + u - 4 + (VLAG - TLAG) + 2)
                    nc.scalar.activation(PTs[:, u % 4, 0:w_of(u) * P], bank[4 + u % 2][:, 0:w_of(u) * P],
                                         ACT.Copy).then_inc(s_pta, 1)

                for i in range(NU + TLAG):
                    if i < NU:
                        u, w = i, w_of(i) * P
                        act.wait_ge(s_sm, lap * NU + u + 1)
                        if u >= 4:
                            act.wait_ge(s_t, lap * NU + u - 3)
                        nc.scalar.activation(PR[:, u % 4, 0:w], SM[:, u % 4, 0:w], ACT.Exp, bias=nb[:, u:u + 1],
                                             scale=-1.0, accum_out=rsum[:, u:u + 1]).then_inc(s_p, 1)
                    if i >= TLAG and (i - TLAG) % 2 == 0:
                        turned(i - TLAG)

            def scores_vector(dve, lap, link, mask, scale, dst, dv):
                def turned(u):
                    dve.wait_ge(s_t, lap * NU + u + 1)
                    if u >= 4:
                        dve.wait_ge(s_t, lap * NU + u - 4 + (VLAG - TLAG) + 2)
                    nc.vector.tensor_copy(PTs[:, u % 4, 0:w_of(u) * P], bank[4 + u % 2][:, 0:w_of(u) * P])\
                        .then_inc(s_ptv, 1)

                def finish(g):
                    dve.wait_ge(s_p, lap * NU + 4 * g + 4)
                    link(nc.vector.reciprocal(rinv[:, 4 * g:4 * g + 4], rsum[:, 4 * g:4 * g + 4]))
                    dve.wait_ge(s_pv, lap * NG + g + 1)
                    nc.vector.tensor_tensor(dst(g), bank[6 + g % 2][:, 0:4 * dv].rearrange("p (q v) -> p q v", q=4),
                                            rinv[:, 4 * g:4 * g + 4].unsqueeze(2).to_broadcast([P, 4, dv]),
                                            ALU.mult).then_inc(s_o, 1)

                for i in range(NU + VLAG + 1):
                    if i < NU:
                        u, w = i, w_of(i) * P
                        dve.wait_ge(s_s, lap * NU + u + 1)
                        if u >= 4:
                            dve.wait_ge(s_p, lap * NU + u - 3)
                        nc.vector.memset(tick[:, u:u + 1], 0.0)
                        nc.vector.tensor_tensor_reduce(out=SM[:, u % 4, 0:w], in0=bank[u % 4][:, 0:w], in1=mask(u),
                                                       scale=scale(u), scalar=3.0e38, op0=ALU.add, op1=ALU.min,
                                                       accum_out=nb[:, u:u + 1]).then_inc(s_sm, 1)
                    if TLAG <= i < NU + TLAG and (i - TLAG) % 2 == 1:
                        turned(i - TLAG)
                    j = i - VLAG - 1
                    if j >= 0 and j % 4 == 3:
                        finish(j // 4)

            return scores_tensor, scores_scalar, scores_vector, s_o, NG

        if 'C' in SEQ:
            at[0] = 0
            CG, CA = 4, 4
            sC_w = sem("C_weights")
            sC_kv = sem("C_keys_values_psum")
            sC_wc = sem("C_group_weights")
            sC_q = sem("C_queries_psum")
            sC_qe = sem("C_keys_and_queries")
            sC_po = sem("C_output")
            sC_bo = sem("C_bias")
            cwq, cwk, cwv = ar(CG, KD, P), ar(KD, P), ar(KD, 16)
            cbq, cbk, cbv = ar(CG), ar(1), ar(16)
            cfc, cbf, cmask = ar(KD, D), ar(D), ar(512)
            C_loads = []
            C_loads.append((cwq[:, :, :, :], d["C_wq"].rearrange("g (k p) e -> p g k e", p=P)))
            C_loads.append((cwk[:, :, :], d["C_wk"].rearrange("(k p) e -> p k e", p=P)))
            C_loads.append((cwv[:, :, :], d["C_wv"].rearrange("(k p) e -> p k e", p=P)))
            C_loads.append((cbq[:, :], d["C_bq"]))
            C_loads.append((cbk[:, :], d["C_bk"]))
            C_loads.append((cbv[:, :], d["C_bv"].partition_broadcast(P)))
            C_loads.append((cfc[:, :, :], d["C_fc"].rearrange("(k p) e -> p k e", p=P)))
            C_loads.append((cbf[:, :], d["C_bf"].partition_broadcast(P)))
            C_loads.append((cmask[:, :], d["C_mask"]))
            QT = ar(B * L)
            KT = ar(B * L)
            V = ar(NT, 16)
            wcur = ar(KD, P)
            bcur = ar(1)
            OC = ar(NT, D)
            c_tensor, c_scalar, c_vector, sC_o, C_NG = attention("C", 64, lambda u: u % 4 + 1, None)

            def C_sync(sp, si, inst):
                if si:
                    sp.wait_ge(s_x, NT * si)
                for dst, src in C_loads:
                    sp.dma_start(dst, src).then_inc(sC_w, 16)

            def C_tensor(pe, si, inst):
                transpose_tensor(pe, NRM[si], XN)
                pe.wait_ge(sC_w, 144)
                for b in range(B):
                    for k in range(KD):
                        last = nc.tensor.matmul(bank[b][:, :], cwk[:, k, :], XT[:, k, b * L:(b + 1) * L],
                                                start=k == 0, stop=k == KD - 1)
                    last.then_inc(sC_kv, 1)
                for T in range(NT):
                    for k in range(KD):
                        last = nc.tensor.matmul(bank[4][:, T * 16:(T + 1) * 16], XT[:, k, T * P:(T + 1) * P],
                                                cwv[:, k, :], start=k == 0, stop=k == KD - 1)
                last.then_inc(sC_kv, 1)
                pe.wait_ge(sC_qe, 4)
                with pe.Fori(0, CG) as g:
                    pe.wait_ge(sC_wc, g + 1)
                    pe.wait_ge(sC_o, g * C_NG + 1)
                    for b in range(B):
                        if b >= 2:
                            pe.wait_ge(sC_qe, g * 4 + b + 3)
                        for k in range(KD):
                            last = nc.tensor.matmul(bank[b % 2][:, :], wcur[:, k, :], XT[:, k, b * L:(b + 1) * L],
                                                    start=k == 0, stop=k == KD - 1)
                        last.then_inc(sC_q, 1)
                    pe.wait_ge(sC_qe, g * 4 + 8)

                    def score(u, dst):
                        b, a, t = u // 16, (u // 4) % 4, u % 4
                        return nc.tensor.matmul(dst, QT[32 * a:32 * a + 16, (4 * b + t) * P:(4 * b + t + 1) * P],
                                                KT[32 * a:32 * a + 16, b * L:b * L + (t + 1) * P], start=True, stop=True)

                    c_tensor(pe, g, score, lambda u, m: V[:, 4 * (u // 16) + m, :], 16)
                transpose_tensor(pe, NRM[si, 1], OC, (sC_o, CG * C_NG + 1))
                for T in range(NT):
                    if T >= 2:
                        pe.wait_ge(s_x, NT * si + T - 1)
                    for k in range(KD):
                        last = nc.tensor.matmul(bank[T % 2][:, 0:D], XT[:, k, T * P:(T + 1) * P], cfc[:, k, :],
                                                start=k == 0, stop=k == KD - 1)
                    last.then_inc(sC_po, 1)

            def C_scalar(act, si, inst):
                norm_scalar(act, NRM[si], 0)
                transpose_scalar(act, NRM[si])
                act.wait_ge(sC_w, 144)
                for b in range(B):
                    act.wait_ge(sC_kv, b + 1)
                    nc.scalar.activation(KT[:, b * L:(b + 1) * L], bank[b][:, :], ACT.Identity, bias=cbk[:, 0:1],
                                         scale=1.0).then_inc(sC_qe, 1)
                with act.Fori(0, CG) as g:
                    act.wait_ge(sC_wc, g + 1)
                    for b in range(B):
                        act.wait_ge(sC_q, g * 4 + b + 1)
                        nc.scalar.activation(QT[:, b * L:(b + 1) * L], bank[b % 2][:, :], ACT.Identity,
                                             bias=bcur[:, 0:1], scale=1.0).then_inc(sC_qe, 1)
                    c_scalar(act, g)
                transpose_scalar(act, NRM[si, 1])

            def C_gpsimd(pool, si, inst):
                pool.wait_ge(sC_w, 144)
                pool.wait_ge(s_xn, NT * (NRM[si][0] + 1))
                for t in range(NT):
                    last = nc.gpsimd.tensor_tensor(X[:, t, :], X[:, t, :], cbf[:, :], ALU.add)
                last.then_inc(sC_bo, 1)
                with pool.Fori(0, CG) as g:
                    pool.wait_ge(sC_qe, g * 4 + 4)
                    nc.gpsimd.tensor_copy(bcur[:, 0:1], cbq[:, bass.ds(g, 1)])
                    nc.gpsimd.tensor_copy(wcur[:, :, :], cwq[:, bass.ds(g, 1), :, :].rearrange("p g k e -> p (g k) e"))\
                        .then_inc(sC_wc, 1)

            def C_vector(dve, si, inst, link):
                norm_vector(dve, NRM[si], NT * si, X, XN)
                dve.wait_ge(sC_w, 144)
                dve.wait_ge(sC_kv, 5)
                nc.vector.tensor_tensor(V, bank[4][:, 0:NT * 16].rearrange("p (t v) -> p t v", t=NT),
                                        cbv[:, :].unsqueeze(1).to_broadcast([P, NT, 16]), ALU.add).then_inc(sC_o, 1)
                with dve.Fori(0, CG) as g:
                    link.enter(g, C_NG)
                    c_vector(dve, g, link, lambda u: cmask[:, 512 - (u % 4 + 1) * P:512], lambda u: -0.25,
                             lambda n: OC[:, 4 * (n // 4):4 * (n // 4) + 4, bass.ds(g * 64 + (n % 4) * 16, 16)], 16)
                    link.leave(CG)
                dve.wait_ge(sC_bo, 1)
                for T in range(NT):
                    dve.wait_ge(sC_po, T + 1)
                    nc.vector.tensor_tensor(X[:, T, :], X[:, T, :], bank[T % 2][:, 0:D], ALU.add).then_inc(s_x, 1)

            W['C'] = dict(scalar=C_scalar, vector=C_vector, tensor=C_tensor, gpsimd=C_gpsimd, sync=C_sync)

        if 'D' in SEQ:
            at[0] = 0
            NH, QK, ROPE, R, QR, QT6 = 16, 96, 64, 32, 682, 6
            sD_w = sem("D_weights")
            sD_s = sem("D_small_weights")
            sD_g = sem("D_key_products")
            sD_ge = sem("D_key_products_scaled")
            sD_l = sem("D_latent_rows_scaled")
            sD_f = sem("D_folded_psum")
            sD_fe = sem("D_folded")
            sD_vo = sem("D_value_products")
            sD_voe = sem("D_value_products_scaled")
            sD_qa = sem("D_query_latent_psum")
            sD_ss = sem("D_query_square_sums")
            sD_sd = sem("D_deviations")
            sD_c = sem("D_latent_psum")
            sD_ce = sem("D_latent")
            sD_cn = sem("D_latent_normed")
            sD_ct = sem("D_latent_turned_psum")
            sD_kt = sem("D_latent_turned")
            sD_kp = sem("D_rotary_psum")
            sD_sw = sem("D_rotary_swapped")
            sD_sn = sem("D_rotary_sines")
            sD_rp = sem("D_rotated")
            sD_wc = sem("D_head_weights")
            sD_ot = sem("D_mixed_turned_psum")
            sD_oe = sem("D_mixed_turned")
            sD_po = sem("D_output")
            qln = sb("D_qln", [P, QT6])
            kvlnb = sb("D_kvlnb", [P, R])
            kvln4 = sb("D_kvln4", [P, 1])
            ckv = sb("D_ckv", [P, KD, QK])
            zer = sb("D_zeros", [P, 512])
            Wf = fold[:, 0:KD * NH * QK].rearrange("p (k c) -> p k c", k=KD)
            Wvo = fold[:, KD * NH * QK:].rearrange("p (j c) -> p j c", c=D)
            rs = sb("D_rs", [P, NT])
            ld("D1", qln[:, :], d["D_qln"], sD_s)
            ld("D2", kvlnb[:, :], d["D_kvln"].partition_broadcast(P), sD_s)
            ld("D3", kvln4[:, :], d["D_kvln4"], sD_s)
            ld("D4", ckv[:, :, :], d["D_ckv"].rearrange("(k p) e -> p k e", p=P), sD_s)
            ld("D5", zer[:, :], d["zeros"], sD_s)
            QBT = ar(QT6, NH * QK)
            qbn = ar(NH // 2, QT6 * P)
            kvbK = ar(NH // 2, R)
            qa = ar(QT6, D)
            owT = ar(NH, D)
            kvbV = ar(NH, R)
            top1 = at[0]
            at[0] = 0
            QTd, KTd = ar(B * L), ar(B * L)
            cos, sin = ar(512), ar(512)
            SW = ar(2, 512)
            wch = ar(KD, QK)
            here = at[0]
            qa2 = ar(KD, QR)
            qjunk = ar(2, 512)
            at[0] = here
            OCd = ar(NT, NH * R)
            OT = ar(2, 512)
            C_ = ar(NT, R)
            CSQ = ar(NT, R)
            css, csd = ar(NT), ar(NT)
            qss = ar(NT, 2)
            d_tensor, d_scalar, d_vector, sD_o, D_NG = attention("D", 16, lambda u: 4, None)

            def D_sync(sp, si, inst):
                if si:
                    sp.wait_ge(s_x, NT * si)
                for j in range(QT6):
                    sp.dma_start(QBT[:, j, :].rearrange("p (h c) -> p h c", h=NH)[:, :, 0:ROPE],
                                 d["D_qbp"][j * P:(j + 1) * P, :, :]).then_inc(sD_w, 16)
                sp.dma_start(qbn, d["D_qbn"]).then_inc(sD_w, 16)
                sp.dma_start(kvbK, d["D_kvbK"]).then_inc(sD_w, 16)
                sp.dma_start(qa, d["D_qa"].rearrange("(j p) e -> p j e", p=P)).then_inc(sD_w, 16)
                sp.dma_start(owT, d["D_ow"].rearrange("(h p) e -> p h e", p=P)).then_inc(sD_w, 16)
                sp.dma_start(kvbV, d["D_kvbV"]).then_inc(sD_w, 16)
                sp.wait_ge(sD_fe, 6)
                sp.wait_ge(sD_voe, 4)
                sp.dma_start(cos[0:ROPE], d["D_cos"]).then_inc(sD_w, 16)
                sp.dma_start(sin[0:ROPE], d["D_sin"]).then_inc(sD_w, 16)
                sp.dma_start(qa2, d["D_qaT"].rearrange("(k p) e -> p k e", p=P)).then_inc(sD_w, 16)

            def D_tensor(pe, si, inst):
                pe.wait_ge(sD_w, 176)
                for h in range(NH):
                    if h >= 4:
                        pe.wait_ge(sD_ge, h - 3)
                    p0 = 64 * (h % 2)
                    for j in range(QT6):
                        last = nc.tensor.matmul(bank[h % 4][:, j * R:(j + 1) * R],
                                                qbn[p0:p0 + 64, h // 2, j * P:(j + 1) * P],
                                                kvbK[p0:p0 + 64, h // 2, :], start=True, stop=True)
                    last.then_inc(sD_g, 1)
                for q in range(4):
                    for a in range(4):
                        last = nc.tensor.matmul(bank[4 + q][32 * a:32 * a + 32, 0:D], kvbV[:, 4 * q + a, :],
                                                owT[:, 4 * q + a, :], start=True, stop=True)
                    last.then_inc(sD_vo, 1)
                pe.wait_ge(sD_l, QT6)
                for k in range(KD):
                    for n in range(3):
                        if k == 1 and n == 1:
                            pe.wait_ge(sD_voe, 4)
                        for j in range(QT6):
                            last = nc.tensor.matmul(bank[3 * k + n][:, :], qa[:, j, k * P:(k + 1) * P],
                                                    QBT[:, j, n * 512:(n + 1) * 512], start=j == 0, stop=j == QT6 - 1)
                        last.then_inc(sD_f, 1)
                pe.wait_ge(sD_voe, 4)
                transpose_tensor(pe, NRM[si], XN)
                pe.wait_ge(sD_s, 80)
                pe.wait_ge(sD_fe, 6)
                for T in range(NT):
                    for k in range(KD):
                        last = nc.tensor.matmul(bank[6][:, T * R:(T + 1) * R], XT[:, k, T * P:(T + 1) * P],
                                                ckv[:, k, ROPE:QK], start=k == 0, stop=k == KD - 1)
                last.then_inc(sD_c, 1)
                for b in range(B):
                    if b >= 2:
                        pe.wait_ge(sD_rp, b - 1)
                    for k in range(KD):
                        last = nc.tensor.matmul(bank[b % 2][0:ROPE, :], ckv[:, k, 0:ROPE], XT[:, k, b * L:(b + 1) * L],
                                                start=k == 0, stop=k == KD - 1)
                    last.then_inc(sD_kp, 1)
                pe.wait_ge(sD_w, 224)
                for T in range(NT):
                    if T >= 1:
                        pe.wait_ge(sD_ss, T)
                    for n, w in ((0, 512), (1, QR - 512)):
                        for k in range(KD):
                            last = nc.tensor.matmul(bank[2 + n][:, 0:w], XT[:, k, T * P:(T + 1) * P],
                                                    qa2[:, k, 512 * n:512 * n + w], start=k == 0, stop=k == KD - 1)
                    last.then_inc(sD_qa, 1)
                pe.wait_ge(sD_cn, 3)
                for b in range(B):
                    if b == 2:
                        pe.wait_ge(sD_kt, 2)
                    for t in range(TB):
                        last = nc.tensor.transpose(bank[4 + b % 2][0:R, t * P:(t + 1) * P], C_[:, TB * b + t, :], ident[:, :])
                    last.then_inc(sD_ct, 1)
                pe.wait_ge(sD_kt, 4)
                pe.wait_ge(sD_rp, 4)
                with pe.Fori(0, NH) as h:
                    pe.wait_ge(sD_wc, h + 1)
                    pe.wait_ge(sD_o, h * D_NG + 1)
                    for b in range(B):
                        if b >= 2:
                            pe.wait_ge(sD_rp, h * 4 + b + 3)
                        for k in range(KD):
                            last = nc.tensor.matmul(bank[b % 2][0:QK, :], wch[:, k, :], XT[:, k, b * L:(b + 1) * L],
                                                    start=k == 0, stop=k == KD - 1)
                        last.then_inc(sD_kp, 1)
                    pe.wait_ge(sD_rp, h * 4 + 8)

                    def score(u, dst):
                        b = u // 4
                        return nc.tensor.matmul(dst, QTd[0:QK, u * P:(u + 1) * P], KTd[0:QK, b * L:(b + 1) * L],
                                                start=True, stop=True)

                    d_tensor(pe, h, score, lambda u, m: C_[:, 4 * (u // 4) + m, :], R)
                pe.wait_ge(sD_o, NH * D_NG + 1)
                for T in range(NT):
                    if T >= 2:
                        pe.wait_ge(sD_oe, T - 1)
                    for k in range(4):
                        last = nc.tensor.transpose(bank[T % 2][:, k * P:(k + 1) * P], OCd[:, T, k * P:(k + 1) * P], ident[:, :])
                    last.then_inc(sD_ot, 1)
                    if T:
                        outp(pe, si, T - 1)
                outp(pe, si, NT - 1)

            def outp(pe, si, T):
                pe.wait_ge(sD_oe, T + 1)
                if T >= 2:
                    pe.wait_ge(s_x, NT * si + T - 1)
                for k in range(4):
                    last = nc.tensor.matmul(bank[2 + T % 2][:, 0:D], OT[:, T % 2, k * P:(k + 1) * P], Wvo[:, k, :],
                                            start=k == 0, stop=k == 3)
                last.then_inc(sD_po, 1)

            def D_scalar(act, si, inst):
                norm_scalar(act, NRM[si], 0)
                transpose_scalar(act, NRM[si])
                act.wait_ge(sD_c, 1)
                nc.scalar.activation(C_.rearrange("p t r -> p (t r)"), bank[6][:, :], ACT.Copy).then_inc(sD_ce, 1)
                for b in range(B):
                    act.wait_ge(sD_kp, b + 1)
                    if b >= 2:
                        act.wait_ge(sD_rp, b - 1)
                    nc.scalar.activation(SW[0:32, b % 2, :], bank[b % 2][32:64, :], ACT.Copy)
                    nc.scalar.activation(SW[32:64, b % 2, :], bank[b % 2][0:32, :], ACT.Copy).then_inc(sD_sw, 1)
                for T in range(NT):
                    act.wait_ge(sD_qa, T + 1)
                    if T >= 1:
                        act.wait_ge(sD_ss, T)
                    nc.scalar.activation(qjunk[:, 0, :], bank[2][:, :], ACT.Square, accum_out=qss[:, T, 0:1])
                    nc.scalar.activation(qjunk[:, 1, 0:QR - 512], bank[3][:, 0:QR - 512], ACT.Square,
                                         accum_out=qss[:, T, 1:2]).then_inc(sD_ss, 1)
                act.wait_ge(sD_cn, 1)
                nc.scalar.activation(csd, css, ACT.Sqrt, bias=epsc[:, 1:2], scale=1.0 / R).then_inc(sD_sd, 1)
                act.wait_ge(sD_cn, 2)
                nc.scalar.activation(rs[:, :], rs[:, :], ACT.Sqrt, bias=epsc[:, 1:2], scale=1.0 / QR).then_inc(sD_sd, 1)
                for b in range(B):
                    act.wait_ge(sD_ct, b + 1)
                    nc.scalar.activation(KTd[64:96, b * L:(b + 1) * L], bank[4 + b % 2][0:R, :], ACT.Copy).then_inc(sD_kt, 1)
                with act.Fori(0, NH) as h:
                    for b in range(B):
                        act.wait_ge(sD_kp, h * 4 + b + 5)
                        act.wait_ge(sD_rp, h * 4 + b + 3)
                        nc.scalar.activation(SW[0:32, b % 2, :], bank[b % 2][32:64, :], ACT.Copy)
                        nc.scalar.activation(SW[32:64, b % 2, :], bank[b % 2][0:32, :], ACT.Copy)
                        nc.scalar.activation(QTd[64:96, b * L:(b + 1) * L], bank[b % 2][64:96, :], ACT.Copy)\
                            .then_inc(sD_sw, 1)
                    d_scalar(act, h)
                for T in range(NT):
                    act.wait_ge(sD_ot, T + 1)
                    if T >= 2:
                        act.wait_ge(sD_po, T - 1)
                    nc.scalar.activation(OT[:, T % 2, :], bank[T % 2][:, :], ACT.Copy).then_inc(sD_oe, 1)

            def D_gpsimd(pool, si, inst):
                for b in range(B):
                    pool.wait_ge(sD_w, 224)
                    pool.wait_ge(sD_sw, b + 1)
                    nc.gpsimd.tensor_tensor(SW[0:64, b % 2, :], SW[0:64, b % 2, :], sin[0:64], ALU.mult).then_inc(sD_sn, 1)
                with pool.Fori(0, NH) as h:
                    pool.wait_ge(sD_rp, h * 4 + 4)
                    nc.gpsimd.tensor_copy(wch, Wf[:, :, bass.ds(h * QK, QK)]).then_inc(sD_wc, 1)
                    for b in range(B):
                        pool.wait_ge(sD_sw, h * 4 + b + 5)
                        nc.gpsimd.tensor_tensor(SW[0:64, b % 2, :], SW[0:64, b % 2, :], sin[0:64], ALU.mult)\
                            .then_inc(sD_sn, 1)

            def D_vector(dve, si, inst, link):
                norm_vector(dve, NRM[si], NT * si, X, XN)
                dve.wait_ge(sD_s, 80)
                dve.wait_ge(sD_w, 176)
                for h in range(NH):
                    dve.wait_ge(sD_g, h + 1)
                    nc.vector.tensor_tensor(QBT[:, :, h * QK + ROPE:(h + 1) * QK],
                                            bank[h % 4][:, 0:QT6 * R].rearrange("p (j r) -> p j r", j=QT6),
                                            kvlnb[:, :].unsqueeze(1).to_broadcast([P, QT6, R]), ALU.mult)\
                        .then_inc(sD_ge, 1)
                dve.wait_ge(sD_ge, NH)
                for j in range(QT6):
                    nc.vector.tensor_scalar(QBT[:, j, :], QBT[:, j, :], qln[:, j:j + 1], None, ALU.mult)\
                        .then_inc(sD_l, 1)
                for q in range(4):
                    dve.wait_ge(sD_vo, q + 1)
                    nc.vector.tensor_scalar(Wvo[:, q, :], bank[4 + q][:, 0:D], kvln4[:, 0:1], None, ALU.mult)\
                        .then_inc(sD_voe, 1)
                for n in range(6):
                    dve.wait_ge(sD_f, n + 1)
                    nc.vector.tensor_copy(Wf[:, n // 3, (n % 3) * 512:(n % 3 + 1) * 512], bank[n][:, :])\
                        .then_inc(sD_fe, 1)

                def rotate(dst, b, n):
                    dve.wait_ge(sD_sw, n)
                    link(nc.vector.tensor_tensor(dst, bank[b % 2][0:64, :], cos[0:64], ALU.mult))
                    dve.wait_ge(sD_sn, n)
                    nc.vector.tensor_tensor(dst, dst, SW[0:64, b % 2, :], ALU.add).then_inc(sD_rp, 1)

                dve.wait_ge(sD_w, 224)
                for b in range(B):
                    rotate(KTd[0:64, b * L:(b + 1) * L], b, b + 1)
                dve.wait_ge(sD_ce, 1)
                link(nc.vector.tensor_tensor(CSQ, C_, C_, ALU.mult))
                nc.vector.tensor_reduce(out=css, in_=CSQ, axis=AX.X, op=ALU.add).then_inc(sD_cn, 1)
                dve.wait_ge(sD_ss, NT)
                nc.vector.tensor_tensor(rs[:, :], qss[:, :, 0], qss[:, :, 1], ALU.add).then_inc(sD_cn, 1)
                dve.wait_ge(sD_sd, 2)
                nc.vector.reciprocal(rs[:, :], rs[:, :])
                link(nc.vector.reciprocal(csd, csd))
                nc.vector.tensor_scalar(rs[:, :], rs[:, :], -(128.0 ** -0.5), None, ALU.mult).then_inc(sD_o, 1)
                nc.vector.tensor_tensor(C_, C_, csd.unsqueeze(2).to_broadcast([P, NT, R]), ALU.mult).then_inc(sD_cn, 1)
                with dve.Fori(0, NH) as h:
                    link.enter(h, B + D_NG)
                    for b in range(B):
                        dve.wait_ge(sD_sw, h * 4 + b + 5)
                        link(nc.vector.tensor_tensor(QTd[0:64, b * L:(b + 1) * L], bank[b % 2][0:64, :], cos[0:64], ALU.mult))
                        dve.wait_ge(sD_sn, h * 4 + b + 5)
                        nc.vector.tensor_tensor(QTd[0:64, b * L:(b + 1) * L], QTd[0:64, b * L:(b + 1) * L],
                                                SW[0:64, b % 2, :], ALU.add).then_inc(sD_rp, 1)
                    d_vector(dve, h, link, lambda u: zer[:, :], lambda u: rs[:, u:u + 1],
                             lambda n: OCd[:, 4 * n:4 * n + 4, bass.ds(h * R, R)], R)
                    link.leave(NH)
                for T in range(NT):
                    dve.wait_ge(sD_po, T + 1)
                    nc.vector.tensor_tensor(X[:, T, :], X[:, T, :], bank[2 + T % 2][:, 0:D], ALU.add).then_inc(s_x, 1)

            W['D'] = dict(scalar=D_scalar, vector=D_vector, tensor=D_tensor, gpsimd=D_gpsimd, sync=D_sync)

        if 'B' in SEQ:
            BH, DK, DV, KO = 32, 48, 96, 64
            QKR = KO + DK
            LEVELS = 7
            HC = P // 2
            s_names = ["const", "tables_pe", "tables_dve", "tables_act", "rowp", "rowe", "rowd",
                       "w1", "w2", "w4", "pj", "tap", "cv", "si", "gp", "gs", "gg", "sq", "ss", "rn", "nm", "kt", "kq", "rb0", "rb1",
                       "gk", "d", "ee", "e", "kk", "qk", "ktp", "vtp", "w0", "kd", "vt",
                       "t0", "t0p", "t1", "ml", "x", "xe", "y", "yt", "ty", "tt",
                       "ks", "r", "u2", "ue", "o", "oe", "sp", "sg", "s", "os", "or", "og", "ot", "ote", "wo", "xa",
                       "w3", "h2", "fin"]
            SLOT = {(0, 2): 0, (0, 4): 1, (1, 2): 2, (1, 4): 3}
            b = {n: sem("B_" + n) for n in s_names}
            at[0] = 0
            rms1, rms2, dtb, alog = ar(KD), ar(KD), ar(BH), ar(BH)
            G, BT, DEC, GC = ar(NT, BH), ar(NT, BH), ar(NT, BH), ar(NT, BH)
            LE, GT, lev, blk, gnb = ar(P), ar(P), ar(LEVELS, P), ar(QKR), ar(DV)
            wqk, wv, wg, wo, cw = ar(KD, QKR), ar(KD, DV), ar(KD, DV), ar(D), ar(8)
            lnq = ar(1)
            top = at[0]
            XR = ar(NT, D)
            wab = ar(KD, 2 * BH)
            Z, AZ, MX, UZ = ar(NT, BH), ar(NT, BH), ar(NT, BH), ar(NT, BH)
            TZ, S1, S2_, PZ = ar(NT, BH), ar(NT, BH), ar(NT, BH), ar(NT, BH)
            GAM, NB_, NBG = ar(NT, BH), ar(NT, BH), ar(NT, BH)
            eA = ar(BH)
            ROW = ar(3, B * L)
            at[0] = top
            CQ, SG = ar(B, L), ar(NT, DV)
            RB = ar(2, 2, L)
            QgT, KbgT, KT_, KbT = ar(B * L), ar(B * L), ar(2, L), ar(2, L)
            Kd, Vt = ar(NT, DK), ar(NT, DV)
            alias = at[0]
            gk, E_, W0 = ar(2, 4, P), ar(2, 4 * P), ar(2, 4 * P)
            Tm, Xm = ar(2, 4, P), ar(2, 4, P)
            ML = ar(2, 4, P)
            CQn = late[:, 0:B * L].rearrange("p (n t) -> p n t", n=B)
            VC = late[:, B * L:2 * B * L].rearrange("p (n t) -> p n t", n=B)
            at[0] = alias
            S_, Sg_, R_, US = ar(4, DV), ar(4, DV), ar(4, DV), ar(2, 4, DV)
            OS, OSQ, OG = ar(2, 4, DV), ar(4, DV), ar(2, 4, DV)
            OTs = ar(2, 4 * P)
            oss, orr = ar(2, 4), ar(2, 4)
            at[0] = top + NT * D
            bw12, bw3 = ar(2, KD, FH), ar(FJ, D)
            PTm = fold[:, 0:2048].rearrange("p (b x) -> p b x", b=B)
            TT = fold[:, 2048:4096].rearrange("p (b c i) -> p b c i", b=B, c=4)
            SQ = fold[:, 2048:3072].rearrange("p (b x) -> p b x", b=2)
            RN = fold[:, 3072:4096].rearrange("p (b x) -> p b x", b=2)
            rows_dram = nc.dram_tensor("B_rows", (BH, 3, B * L), f32, kind="Internal").ap()
            B_consts = [(rms1, d["B_rms1"]), (rms2, d["B_rms2"]), (dtb, d["B_dtb"].partition_broadcast(P)),
                        (alog, d["B_alog"].partition_broadcast(P)), (LE, d["B_LE"]), (GT, d["B_GT"]),
                        (lev, d["B_lev"].rearrange("l p i -> p l i")), (blk[0:QKR], d["B_blk"]),
                        (gnb, d["B_gnorm"].partition_broadcast(P)), (lnq, d["B_lnq"]),
                        (wab, d["B_wab"].rearrange("(k p) c -> p k c", p=P))]
            NC_ = 16 * len(B_consts)

            def made(h, k):
                return k if h is None else h * 8 + 8 + k

            def head_weights(sp, h):
                sp.dma_start(wqk, d["B_wqk"][h].rearrange("h (k p) c -> p (h k) c", p=P)).then_inc(b["w1"], 16)
                sp.dma_start(wv, d["B_wv"][h].rearrange("h (k p) c -> p (h k) c", p=P)).then_inc(b["w1"], 16)
                sp.dma_start(cw, d["B_cw"][h].rearrange("h p c -> p (h c)")).then_inc(b["w1"], 16)

            def gate_weights(sp, h):
                sp.dma_start(wg, d["B_wg"][h].rearrange("h (k p) c -> p (h k) c", p=P)).then_inc(b["w4"], 16)

            def project(pe, h, n):
                pe.wait_ge(b["w1"], 48 if h is None else h * 48 + 96)
                if h is not None or n:
                    pe.wait_ge(b["cv"], made(h, 2 * n))
                for w, r, bk in ((wqk, QKR, 6), (wv, DV, 7)):
                    for k in range(KD):
                        last = nc.tensor.matmul(bank[bk][0:r, :], w[:, k, :], XT[:, k, n * L:(n + 1) * L],
                                                start=k == 0, stop=k == KD - 1)
                    last.then_inc(b["pj"], 1)

            def last_tap(act, h, n):
                A_ = nc.scalar.activation
                act.wait_ge(b["pj"], made(h, 2 * n + 1))
                A_(CQn[0:QKR, n, :], bank[6][0:QKR, :], ACT.Copy, scale=cw[0:QKR, 3:4]).then_inc(b["tap"], 1)
                act.wait_ge(b["pj"], made(h, 2 * n + 2))
                A_(VC[0:DV, n, :], bank[7][0:DV, :], ACT.Copy, scale=cw[0:DV, 7:8]).then_inc(b["tap"], 1)

            def silu(act, h, n):
                A_ = nc.scalar.activation
                act.wait_ge(b["cv"], made(h, 2 * n + 1))
                A_(CQn[0:QKR, n, :], CQn[0:QKR, n, :], ACT.Silu).then_inc(b["si"], 1)
                act.wait_ge(b["cv"], made(h, 2 * n + 2))
                A_(VC[0:DV, n, :], VC[0:DV, n, :], ACT.Silu).then_inc(b["si"], 1)

            def conv(dve, link, h, n):
                for dst, rows, src, col, k in ((CQn, QKR, bank[6], 0, 1), (VC, DV, bank[7], 4, 2)):
                    dve.wait_ge(b["tap"], made(h, 2 * n + k))
                    for far in (1, 2, 3):
                        ins = nc.vector.scalar_tensor_tensor(dst[0:rows, n, far:L], src[0:rows, 0:L - far],
                                                             cw[0:rows, col + 3 - far:col + 4 - far],
                                                             dst[0:rows, n, far:L], ALU.mult, ALU.add)
                        if far < 3:
                            link(ins)
                        else:
                            ins.then_inc(b["cv"], 1)

            def B_sync(sp, si, inst):
                if si:
                    sp.wait_ge(s_x, NT * si)
                for dst, src in B_consts:
                    sp.dma_start(dst, src).then_inc(b["const"], 16)
                for m in range(3):
                    sp.wait_ge(b["rowe"], 4 * m + 4)
                    sp.dma_start(rows_dram[:, m, :], ROW[0:BH, m, :]).then_inc(b["rowd"], 16)
                sp.wait_ge(b["rowd"], 48)
                head_weights(sp, slice(0, 1))
                gate_weights(sp, slice(0, 1))
                with sp.Fori(0, BH) as h:
                    sp.wait_ge(b["si"], h * 8 + 8)
                    head_weights(sp, bass.ds(h + 1, 1))
                    for n in range(B):
                        sp.wait_ge(b["kq"], h * 4 + n + 3)
                        sp.dma_start(RB[KO:QKR, n % 2, :, :], rows_dram[bass.ds(h, 1), 0:2, n * L:(n + 1) * L]
                                     .rearrange("h m t -> (h m) t").partition_broadcast(DK)).then_inc(b[f"rb{n % 2}"], 16)
                        sp.dma_start(RB[0:DK, n % 2, 0, :], rows_dram[bass.ds(h, 1), 2:3, n * L:(n + 1) * L]
                                     .rearrange("h m t -> (h m t)").partition_broadcast(DK)).then_inc(b[f"rb{n % 2}"], 16)
                        if n == 1:
                            sp.wait_ge(b["gs"], h * 4 + 8)
                            gate_weights(sp, bass.ds(h + 1, 1))
                    sp.wait_ge(b["xa"], h * 4 + 1)
                    sp.dma_start(wo[0:DV], d["B_wo"][bass.ds(h, 1)].rearrange("h p c -> p (h c)")).then_inc(b["w2"], 16)
                sp.wait_ge(b["xa"], 4 * BH + 1)
                sp.dma_start(bw12, d["B_w12"].rearrange("m (k p) e -> p (m k) e", p=P)).then_inc(b["w3"], 16)
                sp.dma_start(bw3, d["B_w3"].rearrange("(j p) e -> p j e", p=P)).then_inc(b["w3"], 16)

            def B_tensor(pe, si, inst):
                mm = nc.tensor.matmul
                transpose_tensor(pe, NRM[si, 1], XR)
                pe.wait_ge(b["const"], NC_)
                for T in range(NT):
                    for k in range(KD):
                        last = mm(bank[T // 8][:, (T % 8) * 64:(T % 8 + 1) * 64], XT[:, k, T * P:(T + 1) * P],
                                  wab[:, k, :], start=k == 0, stop=k == KD - 1)
                    if T % 8 == 7:
                        last.then_inc(b["tables_pe"], 1)
                pe.wait_ge(b["tables_dve"], 4)
                Gf = G.rearrange("p t h -> p (t h)")
                mm(bank[2][:, :], LE, Gf, start=True, stop=True).then_inc(b["tables_pe"], 1)
                mm(bank[3][:, :], GT, Gf, start=True, stop=True).then_inc(b["tables_pe"], 1)
                mm(bank[4][0:DK, :], ones[:, 0:DK], Gf, start=True, stop=True).then_inc(b["tables_pe"], 1)
                pe.wait_ge(b["tables_dve"], 5)
                for m, src in enumerate((NB_, NBG, GAM)):
                    for q in range(4):
                        n = 4 * m + q
                        if n >= 2:
                            pe.wait_ge(b["rowe"], n - 1)
                        for t in range(4):
                            last = nc.tensor.transpose(bank[5 + n % 2][0:BH, t * P:(t + 1) * P], src[:, 4 * q + t, :], ident[:, :])
                        last.then_inc(b["rowp"], 1)
                pe.wait_ge(b["rowe"], 12)
                for n in range(B):
                    project(pe, None, n)
                pe.wait_ge(b["cv"], 8)
                with pe.Fori(0, BH) as h:
                    pe.wait_ge(b["w4"], h * 16 + 16)
                    pe.wait_ge(b["xa"], h * 4 + 1)
                    for n in range(B):
                        if n >= 2:
                            pe.wait_ge(b["gs"], h * 4 + n + 3)
                        for t in range(4):
                            for k in range(KD):
                                last = mm(bank[4 + n % 2][:, t * DV:(t + 1) * DV], XT[:, k, (4 * n + t) * P:(4 * n + t + 1) * P],
                                          wg[:, k, :], start=k == 0, stop=k == KD - 1)
                        last.then_inc(b["gp"], 1)
                    pe.wait_ge(b["gs"], h * 4 + 8)
                    for n in range(B):
                        pe.wait_ge(b["sq"], h * 4 + n + 1)
                        mm(bank[4 + n][0:QKR, :], blk[0:QKR, :], SQ[0:QKR, n % 2, :], start=True, stop=True)\
                            .then_inc(b["ss"], 1)
                    pe.wait_ge(b["si"], h * 8 + 8)
                    for n in range(B):
                        if n >= 1:
                            pe.wait_ge(b["vt"], h * 4 + n)
                        for t in range(4):
                            last = nc.tensor.transpose(bank[3][:, t * DV:(t + 1) * DV], VC[0:DV, n, t * P:(t + 1) * P],
                                                       ident[0:DV, 0:DV])
                        last.then_inc(b["vtp"], 1)
                    for p in range(2):
                        for m in range(2):
                            n = 2 * p + m
                            pe.wait_ge(b["gk"], h * 4 + n + 1)
                            if n >= 1:
                                pe.wait_ge(b["ee"], h * 4 + n)
                                if m == 0:
                                    pe.wait_ge(b["tt"], h * 24 + 12)
                            for t in range(4):
                                last = mm(bank[0][:, t * P:(t + 1) * P], gk[:, m, t, :], LE, start=True, stop=True)
                            last.then_inc(b["d"], 1)
                            pe.wait_ge(b["kt"], h * 4 + n + 1)
                            pe.wait_ge(b["kq"], h * 4 + n + 5)
                            if n >= 1:
                                pe.wait_ge(b["kd"], h * 4 + n)
                            if n == 0:
                                pe.wait_ge(b["vt"], h * 4 + 4)
                            for t in range(4):
                                last = mm(bank[1][:, t * P:(t + 1) * P], KT_[0:DK, m, t * P:(t + 1) * P],
                                          KbT[0:DK, m, t * P:(t + 1) * P], start=True, stop=True)
                            last.then_inc(b["kk"], 1)
                            for t in range(4):
                                last = mm(bank[2][:, t * P:(t + 1) * P], KT_[0:DK, m, t * P:(t + 1) * P],
                                          CQ[0:DK, n, t * P:(t + 1) * P], start=True, stop=True)
                            last.then_inc(b["qk"], 1)
                            for t in range(4):
                                last = nc.tensor.transpose(bank[3][:, t * DK:(t + 1) * DK], KT_[0:DK, m, t * P:(t + 1) * P],
                                                           ident[0:DK, 0:DK])
                            last.then_inc(b["ktp"], 1)
                        pe.wait_ge(b["rn"], h * 4 + 4)
                        if p:
                            pe.wait_ge(b["cv"], made(h, 4))
                        for m in range(2):
                            n = 2 * p + m
                            pe.wait_ge(b["t0"], h * 4 + n + 1)
                            for t in range(4):
                                last = nc.tensor.transpose(bank[6 + m][:, t * P:(t + 1) * P], TT[:, n, t, :], ident[:, :])
                            last.then_inc(b["t0p"], 1)
                        pe.wait_ge(b["kd"], h * 4 + 2 * p + 2)
                        for l in range(1, LEVELS):
                            for m in range(2):
                                n, j, i = 2 * p + m, 12 * p + 2 * (l - 1) + m, 10 * p + 2 * (l - 1) + m
                                pe.wait_ge(b["ml"], h * 24 + j + 1)
                                if l == 1:
                                    pe.wait_ge(b["t1"], h * 4 + n + 1)
                                else:
                                    pe.wait_ge(b["ty"], h * 20 + i - 1)
                                    pe.wait_ge(b["xe"], h * 24 + j - 1)
                                for t in range(4):
                                    if l < LEVELS - 1:
                                        last = mm(bank[m][:, t * P:(t + 1) * P], ML[:, m, t, :], Tm[:, m, t, :], start=True, stop=True)
                                    else:
                                        last = mm(bank[m][:, t * HC:(t + 1) * HC], ML[0:HC, m, t, :], Tm[0:HC, m, t, 0:HC],
                                                  start=True, stop=True)
                                last.then_inc(b["x"], 1)
                            for m in range(2):
                                n, j = 2 * p + m, 12 * p + 2 * (l - 1) + m
                                pe.wait_ge(b["xe"], h * 24 + j + 1)
                                if l > 1:
                                    pe.wait_ge(b["tt"], h * 24 + j - 1)
                                if l < LEVELS - 1:
                                    for t in range(4):
                                        last = mm(bank[2 + m][:, t * P:(t + 1) * P], TT[:, n, t, :], Xm[:, m, t, :], start=True, stop=True)
                                    last.then_inc(b["y"], 1)
                                for t in range(4):
                                    if l < LEVELS - 1:
                                        last = mm(bank[4 + m][:, t * P:(t + 1) * P], Xm[:, m, t, :], TT[:, n, t, :], start=True, stop=True)
                                    else:
                                        last = mm(bank[4 + m][0:HC, t * HC:(t + 1) * HC], Xm[:, m, t, 0:HC], TT[:, n, t, HC:P],
                                                  start=True, stop=True)
                                last.then_inc(b["yt"], 1)
                            if (p, l) in SLOT:
                                project(pe, h, SLOT[p, l])
                    pe.wait_ge(b["tt"], h * 24 + 24)
                    for c in range(6):
                        if c < 4:
                            if c:
                                pe.wait_ge(b["s"], h * 3 + c)
                                for n in range(B):
                                    T = 4 * n + c
                                    last = mm(bank[0][:, n * DV:(n + 1) * DV], KbgT[0:DK, T * P:(T + 1) * P], S_[0:DK, n, :],
                                              start=True, stop=True)
                                last.then_inc(b["ks"], 1)
                                pe.wait_ge(b["r"], h * 3 + c)
                            for n in range(B):
                                rhs = R_[:, n, :] if c else Vt[:, 4 * n + c, :]
                                last = mm(bank[1][:, n * DV:(n + 1) * DV], TT[:, n, c, :], rhs, start=True, stop=True)
                            last.then_inc(b["u2"], 1)
                            pe.wait_ge(b["ue"], h * 4 + c + 1)
                            if c >= 2:
                                pe.wait_ge(b["oe"], h * 4 + c - 1)
                            for n in range(B):
                                T = 4 * n + c
                                o = bank[2 + c % 2][:, n * DV:(n + 1) * DV]
                                if c:
                                    mm(o, QgT[0:DK, T * P:(T + 1) * P], S_[0:DK, n, :], start=True, stop=False)
                                last = mm(o, PTm[:, n, c * P:(c + 1) * P], US[:, c % 2, n, :], start=not c, stop=True)
                            last.then_inc(b["o"], 1)
                            if c < 3:
                                for n in range(B):
                                    last = mm(bank[4][0:DK, n * DV:(n + 1) * DV], Kd[:, 4 * n + c, :], US[:, c % 2, n, :],
                                              start=True, stop=True)
                                last.then_inc(b["sp"], 1)
                        e = c - 2
                        if e >= 0:
                            pe.wait_ge(b["og"], h * 4 + e + 1)
                            for n in range(B):
                                last = nc.tensor.transpose(bank[5][0:DV, n * P:(n + 1) * P], OG[:, e % 2, n, :], ident[:, :])
                            last.then_inc(b["ot"], 1)
                            if e == 0:
                                pe.wait_ge(b["w2"], h * 16 + 16)
                                pe.wait_ge(b["cv"], made(h, 8))
                            pe.wait_ge(b["ote"], h * 4 + e + 1)
                            if e:
                                pe.wait_ge(b["xa"], h * 4 + e + 1)
                            for n in range(B):
                                last = mm(bank[6 + n // 2][:, (n % 2) * D:(n % 2 + 1) * D], OTs[0:DV, e % 2, n * P:(n + 1) * P],
                                          wo[0:DV, :], start=True, stop=True)
                            last.then_inc(b["wo"], 1)
                transpose_tensor(pe, NRM[si, 2], XR)
                pe.wait_ge(b["w3"], 32)
                glu_tensor(pe, si, GLU[si], bw12.rearrange("p m k e -> p m k e"), bw3)

            def B_scalar(act, si, inst, alink):
                A_ = nc.scalar.activation
                act.wait_ge(b["const"], NC_)
                norm_scalar(act, NRM[si], 0)
                norm_scalar(act, NRM[si, 1], 0)
                transpose_scalar(act, NRM[si, 1], rms1)
                act.wait_ge(b["tables_dve"], 2)
                for n in range(2):
                    A_(BT[:, 8 * n:8 * n + 8, :], bank[n][:, :].rearrange("p (t c) -> p t c", t=8)[:, :, BH:2 * BH],
                       ACT.Sigmoid).then_inc(b["tables_act"], 1)
                A_(eA, alog, ACT.Exp)
                act.wait_ge(b["tables_dve"], 3)
                A_(UZ, AZ, ACT.Exp, scale=-1.0).then_inc(b["tables_act"], 1)
                act.wait_ge(b["tables_pe"], 5)
                A_(GAM.rearrange("p t h -> p (t h)"), bank[2][:, :], ACT.Exp)
                A_(DEC.rearrange("p t h -> p (t h)"), bank[3][:, :], ACT.Exp)
                A_(GC.rearrange("p t h -> p (t h)")[0:DK], bank[4][0:DK, :], ACT.Exp).then_inc(b["tables_act"], 1)
                for n in range(12):
                    act.wait_ge(b["rowp"], n + 1)
                    A_(ROW[0:BH, n // 4, (n % 4) * 512:(n % 4 + 1) * 512], bank[5 + n % 2][0:BH, :], ACT.Copy).then_inc(b["rowe"], 1)
                act.wait_ge(b["rowd"], 48)
                A_(oss0[:, 0:1], epsc[:, 0:1], ACT.Copy).then_inc(b["gs"], 1)
                for n in range(3):
                    A_(oss0[:, n + 1:n + 2], epsc[:, 0:1], ACT.Copy).then_inc(b["gs"], 1)
                act.wait_ge(b["w1"], 48)
                for n in range(B):
                    last_tap(act, None, n)
                    silu(act, None, n)
                with act.Fori(0, BH) as h:
                    alink.enter(h, 2)
                    for n in range(B):
                        act.wait_ge(b["gp"], h * 4 + n + 1)
                        A_(SG[:, 4 * n:4 * n + 4, :].rearrange("p t v -> p (t v)"), bank[4 + n % 2][:, 0:4 * DV],
                           ACT.Silu).then_inc(b["gs"], 1)
                    for n in range(B):
                        if n >= 2:
                            act.wait_ge(b["ss"], h * 4 + n - 1)
                        if n == 0:
                            act.wait_ge(b["si"], h * 8 + 8)
                        A_(SQ[0:QKR, n % 2, :], CQn[0:QKR, n, :], ACT.Square).then_inc(b["sq"], 1)
                    def factors(*pair):
                        for n in pair:
                            act.wait_ge(b["ss"], h * 4 + n + 1)
                            if n >= 2:
                                act.wait_ge(b["nm"], h * 4 + n - 1)
                            ins = A_(RN[0:QKR, n % 2, :], bank[4 + n][0:QKR, :], ACT.Ln, bias=epsc[0:QKR, 1:2], scale=1.0)
                        alink(ins)
                        for n in pair:
                            A_(RN[0:QKR, n % 2, :], RN[0:QKR, n % 2, :], ACT.Exp, bias=lnq[0:QKR, 0:1], scale=-0.5)\
                                .then_inc(b["rn"], 1)

                    factors(0, 1)

                    def keys(n):
                        act.wait_ge(b["nm"], h * 4 + n + 1)
                        A_(KT_[0:DK, n % 2, :], CQ[KO:QKR, n, :], ACT.Copy).then_inc(b["kt"], 1)

                    for p in range(2):
                        for m in range(2):
                            n = 2 * p + m
                            if p:
                                act.wait_ge(b["ktp"], h * 4 + n - 1)
                            keys(n)
                            act.wait_ge(b["d"], h * 4 + n + 1)
                            A_(E_[:, m, :], bank[0][:, :], ACT.Exp).then_inc(b["ee"], 1)
                        if p == 0:
                            factors(2, 3)
                        for m in range(2):
                            act.wait_ge(b["t0p"], h * 4 + 2 * p + m + 1)
                            A_(Tm[:, m, :, :].rearrange("p t i -> p (t i)"), bank[6 + m][:, :], ACT.Copy).then_inc(b["t1"], 1)
                        for l in range(1, LEVELS):
                            for m in range(2):
                                act.wait_ge(b["x"], h * 24 + 12 * p + 2 * (l - 1) + m + 1)
                                if l < LEVELS - 1:
                                    A_(Xm[:, m, :, :].rearrange("p t i -> p (t i)"), bank[m][:, :], ACT.Copy).then_inc(b["xe"], 1)
                                else:
                                    A_(Xm[:, m, :, 0:HC], bank[m][:, 0:4 * HC].rearrange("p (t i) -> p t i", t=4), ACT.Copy)\
                                        .then_inc(b["xe"], 1)
                            if (p, l) in SLOT:
                                last_tap(act, h, SLOT[p, l])
                            if (p, l - 1) in SLOT:
                                silu(act, h, SLOT[p, l - 1])
                    for c in range(6):
                        if c < 4:
                            act.wait_ge(b["u2"], h * 4 + c + 1)
                            A_(US[:, c % 2, :, :].rearrange("p n v -> p (n v)"), bank[1][:, 0:4 * DV], ACT.Copy).then_inc(b["ue"], 1)
                            act.wait_ge(b["o"], h * 4 + c + 1)
                            if c >= 2:
                                act.wait_ge(b["og"], h * 4 + c - 1)
                            A_(OS[:, c % 2, :, :].rearrange("p n v -> p (n v)"), bank[2 + c % 2][:, 0:4 * DV], ACT.Copy)\
                                .then_inc(b["oe"], 1)
                        if c >= 2:
                            act.wait_ge(b["ot"], h * 4 + c - 1)
                            A_(OTs[0:DV, c % 2, :], bank[5][0:DV, :], ACT.Copy).then_inc(b["ote"], 1)
                    alink.leave(BH)
                norm_scalar(act, NRM[si, 2], 0)
                transpose_scalar(act, NRM[si, 2], rms2)
                glu_scalar(act, GLU[si], ACT.Silu)

            def B_gpsimd(pool, si, inst):
                tt = nc.gpsimd.tensor_tensor
                pool.wait_ge(b["rowd"], 48)
                with pool.Fori(0, BH) as h:
                    pool.wait_ge(b["xa"], h * 4 + 1)
                    for p in range(2):
                        for m in range(2):
                            n = 2 * p + m
                            if p:
                                pool.wait_ge(b["d"], h * 4 + n - 1)
                            tt(gk[:, m, :, :], GT.unsqueeze(1).to_broadcast([P, 4, P]),
                               G[:, 4 * n:4 * n + 4, bass.ds(h, 1)].to_broadcast([P, 4, P]), ALU.mult).then_inc(b["gk"], 1)
                        if p == 0:
                            for n in range(B):
                                pool.wait_ge(b["gs"], h * 4 + n + 5)
                                tt(SG[:, 4 * n:4 * n + 4, :], SG[:, 4 * n:4 * n + 4, :],
                                   gnb.unsqueeze(1).to_broadcast([P, 4, DV]), ALU.mult).then_inc(b["gg"], 1)
                        for m in range(2):
                            n = 2 * p + m
                            pool.wait_ge(b["ee"], h * 4 + n + 1)
                            Ev = E_[:, m, :].rearrange("p (t i) -> p t i", t=4)
                            tt(Ev, Ev, LE.unsqueeze(1).to_broadcast([P, 4, P]), ALU.mult).then_inc(b["e"], 1)
                        for m in range(2):
                            n = 2 * p + m
                            pool.wait_ge(b["w0"], h * 4 + n + 1)
                            Wv = W0[:, m, :].rearrange("p (t i) -> p t i", t=4)
                            tt(ML[:, m, :, :], Wv, lev[:, 0, :].unsqueeze(1).to_broadcast([P, 4, P]), ALU.mult).then_inc(b["fin"], 1)
                            pool.wait_ge(b["fin"], h * 4 + n + 1)
                            tt(TT[:, n, :, :], ML[:, m, :, :], ident[:, :].unsqueeze(1).to_broadcast([P, 4, P]), ALU.add)\
                                .then_inc(b["t0"], 1)
                        for l in range(1, LEVELS):
                            for m in range(2):
                                n, j = 2 * p + m, 12 * p + 2 * (l - 1) + m
                                if l == 1:
                                    pool.wait_ge(b["t0"], h * 4 + n + 1)
                                else:
                                    pool.wait_ge(b["x"], h * 24 + j - 1)
                                Wv = W0[:, m, :].rearrange("p (t i) -> p t i", t=4)
                                tt(ML[:, m, :, :], Wv, lev[:, l, :].unsqueeze(1).to_broadcast([P, 4, P]), ALU.mult)\
                                    .then_inc(b["ml"], 1)
                    for c in range(1, 5):
                        if c < 3:
                            pool.wait_ge(b["s"], h * 3 + c)
                            gc = GC[0:DK, :, bass.ds(h, 1)].rearrange("p (n c) o -> p n (c o)", n=B)[:, :, c:c + 1]
                            tt(Sg_[0:DK], S_[0:DK], gc.to_broadcast([DK, B, DV]), ALU.mult).then_inc(b["sg"], 1)
                        pool.wait_ge(b["os"], h * 4 + c)
                        tt(orr[:, (c - 1) % 2, :], oss[:, (c - 1) % 2, :], mhalf[:, :], ALU.pow).then_inc(b["or"], 1)
                pool.wait_ge(b["xa"], 4 * BH + 1)
                for T in range(NT):
                    last = tt(X[:, T, :], X[:, T, :], XN[:, T, :], ALU.add)
                last.then_inc(b["h2"], 1)

            def B_vector(dve, si, inst, link):
                tt, ts, stt = nc.vector.tensor_tensor, nc.vector.tensor_scalar, nc.vector.scalar_tensor_tensor
                norm_vector(dve, NRM[si], NT * si, X, XN)
                dve.wait_ge(s_xn, NT * (NRM[si][0] + 1))
                norm_vector(dve, NRM[si, 1], 0, XN, XR, rms=True)
                dve.wait_ge(b["const"], NC_)
                for n in range(2):
                    dve.wait_ge(b["tables_pe"], n + 1)
                    tt(Z[:, 8 * n:8 * n + 8, :], bank[n][:, :].rearrange("p (t c) -> p t c", t=8)[:, :, 0:BH],
                       dtb.unsqueeze(1).to_broadcast([P, 8, BH]), ALU.add).then_inc(b["tables_dve"], 1)
                dve.wait_ge(b["tables_dve"], 2)
                ts(MX, Z, 0.0, None, ALU.max)
                stt(AZ, Z, -1.0, Z, ALU.mult, ALU.max).then_inc(b["tables_dve"], 1)
                dve.wait_ge(b["tables_act"], 3)
                link(ts(TZ, UZ, 2.0, None, ALU.add))
                link(nc.vector.reciprocal(TZ, TZ))
                link(tt(S1, UZ, TZ, ALU.mult))
                link(tt(S2_, S1, S1, ALU.mult))
                link(ts(PZ, S2_, 1.0 / 17, None, ALU.mult))
                for k in range(7, 0, -1):
                    link(stt(PZ, PZ, 1.0 / (2 * k + 1), S2_, ALU.add, ALU.mult))
                link(stt(PZ, PZ, 1.0, S1, ALU.add, ALU.mult))
                link(stt(PZ, PZ, 2.0, MX, ALU.mult, ALU.add))
                link(tt(PZ, PZ, eA.unsqueeze(1).to_broadcast([P, NT, BH]), ALU.mult))
                ts(G, PZ, -1.0, -200.0, ALU.mult, ALU.max).then_inc(b["tables_dve"], 1)
                dve.wait_ge(b["tables_act"], 4)
                link(ts(NB_, BT, -1.0, None, ALU.mult))
                tt(NBG, NB_, GAM, ALU.mult).then_inc(b["tables_dve"], 1)
                dve.wait_ge(b["rowd"], 48)
                nc.vector.memset(mhalf[:, :], -0.5)
                for n in range(4):
                    nc.vector.memset(tick0[:, n:n + 1], 0.0).then_inc(b["kq"], 1)
                nc.vector.memset(tick0[:, 4:5], 0.0).then_inc(b["xa"], 1)
                dve.wait_ge(b["w1"], 48)
                for n in range(B):
                    conv(dve, link, None, n)
                with dve.Fori(0, BH) as h:
                    link.enter(h, 4 * 4 + 8 + 8)

                    def rows(n):
                        dve.wait_ge(b["rn"], h * 4 + n + 1)
                        tt(CQ[0:QKR, n, :], CQn[0:QKR, n, :], RN[0:QKR, n % 2, :], ALU.mult).then_inc(b["nm"], 1)
                        dve.wait_ge(b["nm"], h * 4 + n + 1)
                        dve.wait_ge(b[f"rb{n % 2}"], h * 64 + 32 * (n // 2) + 32)
                        tt(KbT[0:DK, n % 2, :], CQ[KO:QKR, n, :], RB[KO:QKR, n % 2, 0, :], ALU.mult)
                        tt(KbgT[0:DK, n * L:(n + 1) * L], CQ[KO:QKR, n, :], RB[KO:QKR, n % 2, 1, :], ALU.mult)
                        tt(QgT[0:DK, n * L:(n + 1) * L], CQ[0:DK, n, :], RB[0:DK, n % 2, 0, :], ALU.mult).then_inc(b["kq"], 1)

                    def turned(n):
                        dve.wait_ge(b["vtp"], h * 4 + n + 1)
                        tt(Vt[:, 4 * n:4 * n + 4, :], bank[3][:, 0:4 * DV].rearrange("p (t v) -> p t v", t=4),
                           BT[:, 4 * n:4 * n + 4, bass.ds(h, 1)].to_broadcast([P, 4, DV]), ALU.mult).then_inc(b["vt"], 1)

                    for n in range(B):
                        turned(n)
                    for p in range(2):
                        for m in range(2):
                            n = 2 * p + m
                            if p:
                                dve.wait_ge(b["qk"], h * 4 + n - 1)
                            rows(n)
                            dve.wait_ge(b["e"], h * 4 + n + 1)
                            dve.wait_ge(b["kk"], h * 4 + n + 1)
                            tt(W0[:, m, :], E_[:, m, :], bank[1][:, :], ALU.mult).then_inc(b["w0"], 1)
                            dve.wait_ge(b["qk"], h * 4 + n + 1)
                            tt(PTm[:, n, :], E_[:, m, :], bank[2][:, :], ALU.mult)
                            dve.wait_ge(b["ktp"], h * 4 + n + 1)
                            tt(Kd[:, 4 * n:4 * n + 4, :], bank[3][:, 0:4 * DK].rearrange("p (t v) -> p t v", t=4),
                               DEC[:, 4 * n:4 * n + 4, bass.ds(h, 1)].to_broadcast([P, 4, DK]), ALU.mult).then_inc(b["kd"], 1)
                        for l in range(1, LEVELS):
                            for m in range(2):
                                n, j, i = 2 * p + m, 12 * p + 2 * (l - 1) + m, 10 * p + 2 * (l - 1) + m
                                flat = lambda v: v.rearrange("p t i -> p (t i)")
                                if l < LEVELS - 1:
                                    dve.wait_ge(b["y"], h * 20 + i + 1)
                                    if l > 1:
                                        dve.wait_ge(b["ty"], h * 20 + i - 1)
                                    tt(flat(Tm[:, m, :, :]), flat(Tm[:, m, :, :]), bank[2 + m][:, :], ALU.add).then_inc(b["ty"], 1)
                                dve.wait_ge(b["yt"], h * 24 + j + 1)
                                if l > 1:
                                    dve.wait_ge(b["tt"], h * 24 + j - 1)
                                if l < LEVELS - 1:
                                    tt(flat(TT[:, n, :, :]), flat(TT[:, n, :, :]), bank[4 + m][:, :], ALU.add).then_inc(b["tt"], 1)
                                else:
                                    nc.vector.tensor_copy(TT[0:HC, n, :, HC:P],
                                                          bank[4 + m][0:HC, 0:4 * HC].rearrange("p (t i) -> p t i", t=4)).then_inc(b["tt"], 1)
                            if (p, l) in SLOT:
                                conv(dve, link, h, SLOT[p, l])
                    every = lambda v, c: v.rearrange("p (n c) v -> p n c v", c=4)[:, :, c, :]
                    for c in range(6):
                        if c < 4:
                            if c:
                                dve.wait_ge(b["ks"], h * 3 + c)
                                tt(R_, every(Vt, c), bank[0][:, 0:4 * DV].rearrange("p (n v) -> p n v", n=4), ALU.add).then_inc(b["r"], 1)
                            if c < 3:
                                dve.wait_ge(b["sp"], h * 3 + c + 1)
                                psS = bank[4][0:DK, 0:4 * DV].rearrange("p (n v) -> p n v", n=4)
                                if c:
                                    dve.wait_ge(b["sg"], h * 2 + c)
                                    tt(S_[0:DK], Sg_[0:DK], psS, ALU.add).then_inc(b["s"], 1)
                                else:
                                    nc.vector.tensor_copy(S_[0:DK], psS).then_inc(b["s"], 1)
                        if 1 <= c <= 4:
                            e = c - 1
                            dve.wait_ge(b["oe"], h * 4 + e + 1)
                            link(tt(OSQ, OS[:, e % 2, :, :], OS[:, e % 2, :, :], ALU.mult))
                            link(nc.vector.tensor_reduce(out=oss[:, e % 2, :], in_=OSQ, axis=AX.X, op=ALU.add))
                            ts(oss[:, e % 2, :], oss[:, e % 2, :], 1.0 / DV, 1e-5, ALU.mult, ALU.add).then_inc(b["os"], 1)
                            dve.wait_ge(b["or"], h * 4 + e + 1)
                            if e == 0:
                                dve.wait_ge(b["gg"], h * 4 + 4)
                            if e >= 2:
                                dve.wait_ge(b["ot"], h * 4 + e - 1)
                            link(tt(OG[:, e % 2, :, :], OS[:, e % 2, :, :],
                                    orr[:, e % 2, :].unsqueeze(2).to_broadcast([P, 4, DV]), ALU.mult))
                            tt(OG[:, e % 2, :, :], OG[:, e % 2, :, :], every(SG, e), ALU.mult).then_inc(b["og"], 1)
                        if c >= 2:
                            e = c - 2
                            dve.wait_ge(b["wo"], h * 4 + e + 1)
                            Xv = XN[:, :, :].rearrange("p (n c) v -> p n c v", c=4)[:, :, e, :]
                            for q in range(2):
                                ins = tt(Xv[:, 2 * q:2 * q + 2, :], Xv[:, 2 * q:2 * q + 2, :],
                                         bank[6 + q][:, :].rearrange("p (n v) -> p n v", n=2), ALU.add)
                                if q:
                                    ins.then_inc(b["xa"], 1)
                                else:
                                    link(ins)
                    link.leave(BH)
                dve.wait_ge(b["xa"], 4 * BH + 1)
                norm_vector(dve, NRM[si, 2], 0, XN, XR, rms=True)
                dve.wait_ge(b["h2"], 1)
                glu_vector(dve, GLU[si])

            mhalf = sb("B_mhalf", [P, 4])
            oss0 = sb("B_tick_s", [P, 4])
            tick0 = sb("B_tick_v", [P, 5])
            W['B'] = dict(scalar=B_scalar, vector=B_vector, tensor=B_tensor, gpsimd=B_gpsimd, sync=B_sync)


        @block.sync
        def _(sp):
            sp.dma_start(X[:, :, :], d["x"].rearrange("b (t p) c -> p (b t) c", p=P)).then_inc(s_x0, 16)
            for dst, src, s in loads:
                sp.dma_start(dst, src).then_inc(s, 16)
            for si, kind, inst in plan:
                if 'sync' in W[kind]:
                    W[kind]['sync'](sp, si, inst)
            sp.wait_ge(s_x, NT * len(plan))
            sp.dma_start(out.rearrange("b (t p) c -> p (b t) c", p=P), X[:, :, :]).then_inc(s_out, 16)
            sp.wait_ge(s_out, 16)

        @block.scalar
        def _(act):
            act.wait_ge(s_const, 48)
            alink = Chain(act, s_act)
            for si, kind, inst in plan:
                W[kind]['scalar'](*((act, si, inst, alink) if kind == 'B' else (act, si, inst)))

        @block.vector
        def _(dve):
            link = Chain(dve, s_dve)
            dve.wait_ge(s_const, 48)
            for si, kind, inst in plan:
                W[kind]['vector'](dve, si, inst, link)

        @block.tensor
        def _(pe):
            pe.wait_ge(s_const, 48)
            for si, kind, inst in plan:
                W[kind]['tensor'](pe, si, inst)

        @block.gpsimd
        def _(pool):
            for si, kind, inst in plan:
                if 'gpsimd' in W[kind]:
                    W[kind]['gpsimd'](pool, si, inst)


def layout(i):
    import numpy as np
    a = {k: np.asarray(v) for k, v in i.items()}
    z = lambda *s: np.zeros(s, np.float32)
    r = {"x": a["L0_attn_a_x"]}
    r["ones"] = np.ones((128, 512), np.float32)
    r["ident"] = np.eye(128, dtype=np.float32)
    eps = z(128, 8)
    eps[:, 0] = 1e-5
    eps[:, 1] = 1e-6
    r["eps"] = eps
    if 'A' in SEQ:
        r["A_wqkv"] = np.stack([a[f"L0_attn_a_W{m}"].T for m in "qkv"])
        r["A_wo"] = a["L0_attn_a_Wo"].T
        r["A_b"] = np.stack([a[f"L0_attn_a_b{m}"].reshape(2, 128).T for m in "qkv"], 1)
        r["A_bo"] = a["L0_attn_a_bo"]
    if 'F' in SEQ or 'B' in SEQ:
        r["F_w12"] = np.stack([a["L0_ffn_w1"].T, a["L0_ffn_w2"].T])
        r["F_w3"] = np.concatenate([a["L0_ffn_w3"].T, z(64, 256)])
    if 'E' in SEQ:
        r["E_W1"] = a["L1_ffn_W1"]
        r["E_W2"] = a["L1_ffn_W2"]
        r["E_b1"] = a["L1_ffn_b1"].reshape(8, 128).T
        r["E_b2"] = a["L1_ffn_b2"]
        r["E_Wr"] = a["L1_ffn_W_r"].reshape(256)
        r["E_br"] = a["L1_ffn_b_r"]
        r["iota"] = np.arange(128, dtype=np.float32)
        r["E_off"] = np.array([[0], [64], [0], [64]], np.float32)
    if 'C' in SEQ:
        w, b = a["L1_attn_a_w_qkv"], a["L1_attn_a_b_qkv"]
        r["C_wq"] = np.concatenate([w[:, :256].reshape(256, 16, 16), z(256, 16, 16)], 2).reshape(256, 4, 128).transpose(1, 0, 2)
        r["C_bq"] = np.concatenate([b[:256].reshape(16, 16), z(16, 16)], 1).reshape(4, 128).T
        r["C_wk"] = np.concatenate([w[:, 256:272], z(256, 16)] * 4, 1)
        r["C_bk"] = np.concatenate([b[256:272], z(16)] * 4)[:, None]
        r["C_wv"] = w[:, 272:]
        r["C_bv"] = b[272:]
        r["C_fc"] = a["L1_attn_a_w_fc"]
        r["C_bf"] = a["L1_attn_a_b_fc"]
        r["C_mask"] = np.where(np.arange(512)[None, :] - 384 > np.arange(128)[:, None], np.float32(-1e30), np.float32(0))
    if 'D' in SEQ:
        turn = np.concatenate([np.arange(0, 64, 2), np.arange(1, 64, 2)])
        qb = a["L1_attn_b_q_b_w"].reshape(16, 128, 682)
        pad = lambda v: np.concatenate([v, z(86, *v.shape[1:])])
        r["D_qbp"] = pad(qb[:, 64:, :][:, turn, :].transpose(2, 0, 1))
        qn = np.concatenate([qb[:, :64, :], z(16, 64, 86)], 2)
        r["D_qbn"] = qn.reshape(8, 2, 64, 768).transpose(1, 2, 0, 3).reshape(128, 8, 768)
        kvb = a["L1_attn_b_kv_b_w"].reshape(16, 192, 32)
        r["D_kvbK"] = kvb[:, :64].reshape(8, 2, 64, 32).transpose(1, 2, 0, 3).reshape(128, 8, 32)
        r["D_kvbV"] = kvb[:, 64:].transpose(1, 0, 2)
        r["D_qa"] = pad(a["L1_attn_b_q_a_w"])
        r["D_qaT"] = a["L1_attn_b_q_a_w"].T
        r["D_ow"] = a["L1_attn_b_o_w"].T
        r["D_qln"] = pad(a["L1_attn_b_q_a_ln"]).reshape(6, 128).T
        r["D_kvln"] = a["L1_attn_b_kv_a_ln"]
        r["D_kvln4"] = np.concatenate([a["L1_attn_b_kv_a_ln"]] * 4)[:, None]
        kva = a["L1_attn_b_kv_a_w"]
        r["D_ckv"] = np.concatenate([kva[32:][turn], kva[:32]]).T
        inv = (np.float32(1.0) / np.float32(128000.0) ** (np.arange(0, 64, 2, dtype=np.float32) / np.float32(64))).astype(np.float32)
        ang = inv[:, None] * np.arange(512, dtype=np.float32)[None, :]
        r["D_cos"] = np.concatenate([np.cos(ang)] * 2).astype(np.float32)
        r["D_sin"] = np.concatenate([-np.sin(ang), np.sin(ang)]).astype(np.float32)
        r["zeros"] = z(128, 512)
    if 'B' in SEQ:
        g = lambda n: a["L0_attn_b_" + n]
        r["B_rms1"], r["B_rms2"] = g("rms1_w").reshape(2, 128).T, g("rms2_w").reshape(2, 128).T
        r["B_dtb"], r["B_alog"], r["B_gnorm"] = g("dt_bias"), g("A_log"), g("gnorm_w")
        ii = np.arange(128)
        r["B_LE"] = (ii[:, None] <= ii[None, :]).astype(np.float32)
        r["B_GT"] = (ii[:, None] > ii[None, :]).astype(np.float32)
        j, i = ii[:, None], ii[None, :]
        r["B_lev"] = np.stack([((j >> (l + 1)) == (i >> (l + 1))) & ((j >> l) % 2 == 0) & ((i >> l) % 2 == 1)
                               for l in range(7)]).astype(np.float32)
        q = np.arange(112)
        part = np.where(q < 48, 0, np.where(q < 64, 1, 2))
        r["B_blk"] = (part[:, None] == part[None, :]).astype(np.float32)
        r["B_lnq"] = np.where(ii < 48, np.float32(-0.5 * np.log(48.0)), np.float32(0))[:, None].astype(np.float32)
        r["B_wab"] = np.concatenate([g("Wa"), g("Wb")], 1)
        heads = lambda w, n: w.reshape(256, 32, n).transpose(1, 0, 2)
        r["B_wqk"] = np.concatenate([heads(g("Wq"), 48), z(32, 256, 16), heads(g("Wk"), 48)], 2)
        r["B_wv"], r["B_wg"] = heads(g("Wv"), 96), heads(g("Wg"), 96)
        for k in ("B_wqk", "B_wv", "B_wg"):
            r[k] = np.concatenate([r[k], z(1, *r[k].shape[1:])])
        r["B_wo"] = g("Wo").reshape(32, 96, 256)
        cqk = np.concatenate([g("conv_q_w").reshape(32, 48, 4), z(32, 16, 4), g("conv_k_w").reshape(32, 48, 4), z(32, 16, 4)], 1)
        cv = np.concatenate([g("conv_v_w").reshape(32, 96, 4), z(32, 32, 4)], 1)
        r["B_cw"] = np.concatenate([np.concatenate([cqk, cv], 2), z(1, 128, 8)])
        r["B_w12"] = np.stack([g("W1"), g("W3")])
        r["B_w3"] = np.concatenate([g("W2"), z(64, 256)])
    return {k: np.ascontiguousarray(v) for k, v in r.items()}


def kernel(**inputs):
    import concourse.bacc as _bacc
    from concourse import mybir as _mybir
    from concourse.bass_utils import run_bass_kernel_spmd as _run

    nc = _bacc.Bacc("TRN2", target_bir_lowering=False, num_devices=1)
    arrays = {f"in_{k}": v for k, v in layout(inputs).items()}
    d = {k[3:]: nc.dram_tensor(k, v.shape, _mybir.dt.from_np(v.dtype), kind="ExternalInput").ap()
         for k, v in arrays.items()}
    out = nc.dram_tensor("out_x", (4, 512, 256), _mybir.dt.float32, kind="ExternalOutput").ap()
    build(nc, d, out)
    r = _run(nc, [arrays], core_ids=[0])
    return r.results[0]["out_x"]
```
